# Optimizing a Trainium2 kernel written in Bass

```python
import numpy as np
import jax
import jax.numpy as jnp

def _softmax(x, axis=-1):
    return jax.nn.softmax(x, axis=axis)

def _gelu(x):
    return jax.nn.gelu(x, approximate=True)

def _silu(x):
    return jax.nn.silu(x)

def _sigmoid(x):
    return jax.nn.sigmoid(x)

def _layernorm(x, axis=-1, eps=1e-05):
    m = jnp.mean(x, axis=axis, keepdims=True)
    v = jnp.var(x, axis=axis, keepdims=True)
    return (x - m) / jnp.sqrt(v + eps)

def _scatter_add(tgt, idx, src, axis=0):
    return tgt.at[idx].add(src)

def _segment_sum(src, seg, n):
    return jax.ops.segment_sum(src, seg, n)
kernel_name = 'mk_gnn_preln_d1_gnn_r32_331491'

def setup_inputs(seed: int=0):
    np.random.seed(seed)
    _w = jnp.asarray

    def _rec_inputs():
        import jax
        import jax.numpy as jnp
        _gk = jax.random.key(seed)
        x = -8.776e-05 + 1 * jax.random.normal(jax.random.fold_in(_gk, 1), (3125, 256), jnp.float32)
        src = jax.random.randint(jax.random.fold_in(_gk, 2), (50000,), 0, 3125, jnp.int32)
        dst = jnp.minimum((3125 * jax.random.uniform(jax.random.fold_in(_gk, 3), (50000,)) ** 2.0).astype(jnp.int32), 99999)
        _o = jnp.argsort(dst, stable=True)
        src = src[_o]
        dst = dst[_o]
        edge_attr_64 = 0.000279952 + 1.00013 * jax.random.normal(jax.random.fold_in(_gk, 11), (50000, 64), jnp.float32)
        return (x, src, dst, edge_attr_64)
    x, src, dst, edge_attr_64 = _rec_inputs()

    def _L0_gnn_setup():
        import jax, jax.numpy as jnp
        import numpy as np
        N, E, H, ED = (625, 10000, 256, 64)
        key = jax.random.key(seed)
        ks = jax.random.split(key, 12)

        def init_w(k, shape, fan_in):
            return (jax.random.normal(k, shape, jnp.float32) / np.sqrt(fan_in)).astype(jnp.float32)
        h = jax.random.normal(ks[0], (N, H), jnp.float32)
        edge_indices = jax.random.randint(ks[1], (2, E), 0, N, jnp.int32)
        edge_attr = jax.random.normal(ks[2], (E, ED), jnp.float32)
        din = 2 * H + ED
        W1 = init_w(ks[3], (H, din), din)
        b1 = jnp.zeros((H,), jnp.float32)
        W2 = init_w(ks[4], (H, H), H)
        b2 = jnp.zeros((H,), jnp.float32)
        W_ih = init_w(ks[5], (3 * H, H), H)
        b_ih = jnp.zeros((3 * H,), jnp.float32)
        W_hh = init_w(ks[6], (3 * H, H), H)
        b_hh = jnp.zeros((3 * H,), jnp.float32)
        return {'h': h, 'edge_indices': edge_indices, 'edge_attr': edge_attr, 'W1': W1, 'b1': b1, 'W2': W2, 'b2': b2, 'W_ih': W_ih, 'b_ih': b_ih, 'W_hh': W_hh, 'b_hh': b_hh}
    _L0_gnn_all = _L0_gnn_setup()
    _L0_gnn_in = {k: v for k, v in _L0_gnn_all.items() if k in ('W1', 'b1', 'W2', 'b2', 'W_ih', 'b_ih', 'W_hh', 'b_hh')}
    del _L0_gnn_all
    return {'x': x, 'src': src, 'dst': dst, 'edge_attr_64': edge_attr_64, 'L0_gnn_W1': _L0_gnn_in['W1'], 'L0_gnn_b1': _L0_gnn_in['b1'], 'L0_gnn_W2': _L0_gnn_in['W2'], 'L0_gnn_b2': _L0_gnn_in['b2'], 'L0_gnn_W_ih': _L0_gnn_in['W_ih'], 'L0_gnn_b_ih': _L0_gnn_in['b_ih'], 'L0_gnn_W_hh': _L0_gnn_in['W_hh'], 'L0_gnn_b_hh': _L0_gnn_in['b_hh']}

def reference(x, src, dst, edge_attr_64, L0_gnn_W1, L0_gnn_b1, L0_gnn_W2, L0_gnn_b2, L0_gnn_W_ih, L0_gnn_b_ih, L0_gnn_W_hh, L0_gnn_b_hh):
    import jax
    import jax.numpy as jnp

    def _L0_gnn_ref(h, edge_indices, edge_attr, W1, b1, W2, b2, W_ih, b_ih, W_hh, b_hh):
        import jax, jax.numpy as jnp
        import numpy as np
        N, E, H, ED = (625, 10000, 256, 64)
        row, col = (edge_indices[0], edge_indices[1])
        edge_in = jnp.concatenate([h[row], h[col], edge_attr], axis=-1)
        msg = jax.nn.relu(edge_in @ W1.T + b1) @ W2.T + b2
        agg = jax.ops.segment_sum(msg, row, num_segments=h.shape[0])
        gx = agg @ W_ih.T + b_ih
        gh = h @ W_hh.T + b_hh
        xr, xz, xn = jnp.split(gx, 3, axis=-1)
        hr, hz, hn = jnp.split(gh, 3, axis=-1)
        r = jax.nn.sigmoid(xr + hr)
        z = jax.nn.sigmoid(xz + hz)
        n = jnp.tanh(xn + r * hn)
        h_new = (1.0 - z) * n + z * h
        return h_new
    edge_index = jnp.stack([src, dst])
    h = jnp.maximum(_layernorm(x, axis=-1), 0.0)
    x = x + _L0_gnn_ref(h, edge_index, edge_attr_64, L0_gnn_W1, L0_gnn_b1, L0_gnn_W2, L0_gnn_b2, L0_gnn_W_ih, L0_gnn_b_ih, L0_gnn_W_hh, L0_gnn_b_hh)
    return x

_drawn_inputs = setup_inputs


def setup_inputs(seed=0):
    import zlib

    import numpy as np

    out = dict(_drawn_inputs(seed))
    spreads = {'L0_gnn_b1': (0.0, 0.1),
     'L0_gnn_b2': (0.0, 0.1),
     'L0_gnn_b_ih': (0.0, 0.537),
     'L0_gnn_b_hh': (0.0, 0.655)}
    factors = {}
    for name, (base, spread) in spreads.items():
        noise = np.random.default_rng([zlib.crc32(name.encode()), seed]).standard_normal(out[name].shape)
        drawn = base * np.exp(spread * noise) if base else spread * noise
        out[name] = jnp.asarray(drawn.astype(out[name].dtype))
    for name, factor in factors.items():
        out[name] = (out[name] * factor).astype(out[name].dtype)
    return out
```

```python
import concourse.bass as bass
from concourse import mybir
from contextlib import ExitStack

F32 = mybir.dt.float32
F32R = mybir.dt.float32r
BF16 = mybir.dt.bfloat16
I32 = mybir.dt.int32
ALU = mybir.AluOpType
ACT = mybir.ActivationFunctionType

P = 128
NODES, EDGES, H, ED = 3125, 50000, 256, 64
G3 = 3 * H
NB = -(-NODES // P)
NODES_PAD = NB * P
EC = -(-EDGES // P)
EDGES_PAD = EC * P
BINS = NB + 1
CH = 16
FULL = EC // CH
CH_LAST = EC - FULL * CH
UN = 16
NT = -(-((EDGES + NB * (P - 1)) // P) // UN) * UN
SLOTS = NT * P
GRP = 4
NGRP = UN // GRP
NG = 8
ROW = 2 * ED + 2
SW = H + 2
GW = G3 + H
EPS = 1e-5
CLEAR = 13
assert FULL == NB - 1 and FULL % 2 == 0 and (SLOTS // P) % CLEAR == 0


def gnn_layer(nc, x, src, dst, ea, w1pq, w1c, w2, wih, whh, b1, b2, bih, bhh, out):
    ctx = ExitStack()
    with ctx:
        def sb(name, shape, dt=F32):
            return ctx.enter_context(nc.sbuf_tensor(name, shape, dt))

        def sem(name):
            return ctx.enter_context(nc.semaphore(name))

        sorted_rows = nc.dram_tensor("sorted_rows", [SLOTS + P, ROW], F32, kind="Internal").ap()
        q_table = nc.dram_tensor("q_table", [NODES_PAD, H], F32, kind="Internal").ap()
        spill = nc.dram_tensor("spill", [NODES_PAD, GW], F32, kind="Internal").ap()

        ident = sb("ident", [P, P])
        ones = sb("ones", [P, P])
        below = sb("below", [P, P])
        ones_cols = sb("ones_cols", [P, EC], BF16)
        iota_i = sb("iota_i", [P, NT], I32)
        iota_f = sb("iota_f", [P, NT])
        eps_t = sb("eps_t", [P, 1])
        w1pq_s = sb("w1pq_s", [P, 2, 2 * H])
        w1c_s = sb("w1c_s", [P, H])
        w1c_hi = sb("w1c_hi", [P, H], F32R)
        w1c_lo = sb("w1c_lo", [P, H], F32R)
        w2_s = sb("w2_s", [P, 2, H])
        wih_s = sb("wih_s", [P, 2, G3])
        whh_s = sb("whh_s", [P, 2, G3])
        wc_s = sb("wc_s", [P, 2, G3])
        cb_s = sb("cb_s", [2, G3])
        b1_s = sb("b1_s", [P, H])
        bhh_s = sb("bhh_s", [P, G3])
        b2_s = sb("b2_s", [P, 2])

        src_i = sb("src_i", [P, EC], I32)
        dst_i = sb("dst_i", [P, EC], I32)
        tmp_i = sb("tmp_i", [P, EC], I32)
        bin_f = sb("bin_f", [P, EC])
        loc_f = sb("loc_f", [P, EC])
        pos_f = sb("pos_f", [P, EC])
        pos_i = sb("pos_i", [P, EC], I32)
        ranked = sb("ranked", [P, 2, EC])
        hit = sb("hit", [P, 2, EC])
        counts = sb("counts", [P, BINS])
        tiles_i = sb("tiles_i", [P, BINS], I32)
        tiles_f = sb("tiles_f", [P, BINS])
        tiles_end = sb("tiles_end", [P, BINS])
        tile_start = sb("tile_start", [P, BINS])
        base = sb("base", [P, BINS])
        blk_f = sb("blk_f", [1, NT])
        off_p = sb("off_p", [1, NT], I32)
        off_s = sb("off_s", [1, NT], I32)

        xs = sb("xs", [P, NB * SW])
        x_blk = xs[:, 0:NB * H]
        stats = sb("stats", [P, NB, 6])
        mv = sb("mv", [P, NB, 2])
        rstd = sb("rstd", [P, NB])
        nmr = sb("nmr", [P, NB])

        p_tab = sb("p_tab", [P, NB * 2 * H], F32R)
        hT = sb("hT", [P, 2, P])
        p_tmp = sb("p_tmp", [P, H])
        q_tmp = sb("q_tmp", [P, H])
        g_tmp = sb("g_tmp", [P, GW])
        ea_in = sb("ea_in", [P, 2, CH, ED])
        rows = sb("rows", [P, 2, CH, ROW])
        slot_i = sb("slot_i", [P, 2, CH], I32)

        oh = sb("oh", [P, 8, P])
        tT = sb("tT", [P, 4, 2 * P], F32R)
        arena = sb("arena", [P, 6786])

        def cut(at, *dims):
            n = 1
            for d in dims:
                n *= d
            names = " ".join("abc"[:len(dims)])
            v = arena[:, at:at + n]
            return v if len(dims) == 1 else v.rearrange(
                f"p ({names}) -> p {names}", **{c: d for c, d in zip("abc", dims)})

        mask = cut(0, BINS * EC // 2).bitcast(BF16)
        cleared = cut(5096, CLEAR, ROW)
        srt = cut(0, NGRP, GRP * ROW)
        gath = cut(2080, NG, H)
        pre = cut(4128, 4, H)
        m_t = cut(5152, 4, SW)
        x_in = cut(0, 2, H)
        g_in = cut(512, 2, GW)
        s_in = cut(2560, 2, SW)
        sT = cut(3076, 2, H)
        cT = cut(3588, 2, P)
        rz = cut(3844, 2, 2 * H)
        nn = cut(4868, 2, H)
        upd = cut(5380, 2, H)
        o_t = cut(5892, 2, H)

        bank = [ctx.enter_context(nc.psum_tensor(f"bank{i}", [P, 512], F32)) for i in range(8)]
        ps_tr, ps_pre, ps_seg = bank[0:2], bank[2:6], bank[6:8]

        src_in, dst_in, x_loaded = sem("src_in"), sem("dst_in"), sem("x_loaded")
        w_loaded = sem("w_loaded")
        cleared_made, slots_cleared = sem("cleared_made"), sem("slots_cleared")
        pool_step, dve_step, act_step = sem("pool_step"), sem("dve_step"), sem("act_step")
        consts_ready = sem("consts_ready")
        pool_waited = sem("pool_waited")
        counted, summed = sem("counted"), sem("summed")
        hit_ready, hit_added = sem("hit_ready"), sem("hit_added")
        placed = sem("placed")
        var_ready, std_ready, norm_ready = sem("var_ready"), sem("std_ready"), sem("norm_ready")
        wc_psum, wc_ready = sem("wc_psum"), sem("wc_ready")
        w1c_ready = sem("w1c_ready")
        ea_loaded = [sem(f"ea_loaded{r}") for r in range(2)]
        hi_built, rows_built = sem("hi_built"), sem("rows_built")
        scattered = [sem(f"scattered{r}") for r in range(2)]
        h_ready, hT_psum, hT_ready = sem("h_ready"), sem("hT_psum"), sem("hT_ready")
        pq_psum, gh_psum = sem("pq_psum"), sem("gh_psum")
        p_ready, p_hi, p_done = sem("p_ready"), sem("p_hi"), sem("p_done")
        q_ready, gh_ready = sem("q_ready"), sem("gh_ready")
        q_stored, g_stored = sem("q_stored"), sem("g_stored")
        tabs_ready = sem("tabs_ready")
        m_init, s_init = sem("m_init"), sem("s_init")
        srt_loaded = [sem(f"srt_loaded{g}") for g in range(NGRP)]
        gathered = [sem(f"gathered{g}") for g in range(NG)]
        oh_ready, tr_psum, tT_ready = sem("oh_ready"), sem("tr_psum"), sem("tT_ready")
        pre_psum, pre_ready, m_ready = sem("pre_psum"), sem("pre_ready"), sem("m_ready")
        seg_psum, s_added = sem("seg_psum"), sem("s_added")
        xg_loaded = [sem(f"xg_loaded{r}") for r in range(2)]
        s_copied, sT_psum, sT_ready = sem("s_copied"), sem("sT_psum"), sem("sT_ready")
        gx_psum, rz_sum, rz_ready = sem("gx_psum"), sem("rz_sum"), sem("rz_ready")
        n_sum, n_ready, zd_ready = sem("n_sum"), sem("n_ready"), sem("zd_ready")
        o_ready = sem("o_ready")
        o_stored = [sem(f"o_stored{r}") for r in range(2)]

        block = ctx.enter_context(nc.Block())

        SCAT = 16 * CH
        ea_v = ea.rearrange("(p c) d -> p c d", p=P)
        sorted_v = sorted_rows[0:SLOTS, :].rearrange("(t p) c -> p t c", p=P)
        x_v = x.rearrange("(b p) f -> p b f", p=P)
        q_v = q_table.rearrange("(b p) f -> p b f", p=P)
        spill_v = spill.rearrange("(b p) f -> p b f", p=P)
        out_v = out.rearrange("(b p) f -> p b f", p=P)
        N_W = 11

        @block.sync
        def _(sp):
            sp.dma_start(src_i[:, :], src.rearrange("(p c) -> p c", p=P)).then_inc(src_in, 16)
            sp.dma_start(x_blk.rearrange("p (b f) -> p b f", b=NB), x_v).then_inc(x_loaded, 16)
            sp.dma_start(dst_i[:, :], dst.rearrange("(p c) -> p c", p=P)).then_inc(dst_in, 16)
            for tile_, view in (
                (w1pq_s[:, :, :], w1pq.rearrange("(c p) n -> p c n", p=P)),
                (w1c_s[0:ED, :], w1c), (w1c_s[ED:2 * ED, :], w1c),
                (w2_s[:, :, :], w2.rearrange("(c p) n -> p c n", p=P)),
                (wih_s[:, :, :], wih.rearrange("(c p) n -> p c n", p=P)),
                (whh_s[:, :, :], whh.rearrange("(c p) n -> p c n", p=P)),
                (b1_s[:, :], b1.rearrange("(a n) -> a n", a=1).to_broadcast([P, H])),
                (bhh_s[:, :], bhh.rearrange("(a n) -> a n", a=1).to_broadcast([P, G3])),
                (b2_s[:, 0:1], b2[0:P].rearrange("(p a) -> p a", a=1)),
                (b2_s[:, 1:2], b2[P:2 * P].rearrange("(p a) -> p a", a=1)),
                (cb_s[1:2, :], bih.rearrange("(a n) -> a n", a=1)),
            ):
                sp.dma_start(tile_, view).then_inc(w_loaded, 16)
            for r in range(2):
                sp.dma_start(ea_in[:, r, :, :], ea_v[:, r * CH:(r + 1) * CH, :]).then_inc(ea_loaded[r], 16)
            sp.wait_ge(cleared_made, 2)
            reps = SLOTS // P // CLEAR
            sp.dma_start(
                sorted_rows[0:SLOTS, :].rearrange("(p a r) c -> p a (r c)", p=P, a=reps),
                cleared.rearrange("p r c -> p (r c)").unsqueeze(1).to_broadcast([P, reps, CLEAR * ROW]),
            ).then_inc(slots_cleared, 16)
            with sp.Fori(1, FULL // 2) as it:
                for r in range(2):
                    sp.wait_ge(rows_built, 2 * it + r - 1)
                    sp.dma_start(ea_in[:, r, :, :], ea_v[:, bass.ds(it * (2 * CH) + r * CH, CH), :]
                                 ).then_inc(ea_loaded[r], 16)
            sp.wait_ge(rows_built, FULL - 1)
            sp.dma_start(ea_in[:, 0, 0:CH_LAST, :], ea_v[:, FULL * CH:EC, :]).then_inc(ea_loaded[0], 16)

            sp.wait_ge(scattered[0], SCAT * (FULL // 2) + 16 * CH_LAST)
            sp.wait_ge(scattered[1], SCAT * (FULL // 2))

            def load_group(turn, g):
                sp.dma_start(srt[:, g, :].rearrange("p (t c) -> p t c", t=GRP),
                             sorted_v[:, bass.ds(turn * UN + g * GRP, GRP), :]).then_inc(srt_loaded[g], 16)

            for g in range(NGRP):
                load_group(0, g)
            with sp.Fori(1, NT // UN) as turn:
                for g in range(NGRP):
                    sp.wait_ge(pre_ready, turn * UN + (g + 1) * GRP - UN)
                    load_group(turn, g)

            sp.wait_ge(s_added, NT)
            sp.wait_ge(g_stored, 16 * NB)

            def load_block(b, r):
                sp.dma_start(x_in[:, r, :], x_v[:, bass.ds(b, 1), :].rearrange("p b f -> p (b f)")
                             ).then_inc(xg_loaded[r], 16)
                sp.dma_start(g_in[:, r, :], spill_v[:, bass.ds(b, 1), :].rearrange("p b f -> p (b f)")
                             ).then_inc(xg_loaded[r], 16)

            def store_block(b, r, b_next):
                sp.wait_ge(o_ready, b_next)
                sp.dma_start(out_v[:, bass.ds(b, 1), :].rearrange("p b f -> p (b f)"), o_t[:, r, :]
                             ).then_inc(o_stored[r], 16)

            load_block(0, 0)
            load_block(1, 1)
            with sp.Fori(0, NB // 2 - 1) as it:
                for r in range(2):
                    store_block(2 * it + r, r, 2 * it + (r + 1))
                    load_block(2 * it + (r + 2), r)
            store_block(NB - 3, 0, NB - 2)
            load_block(NB - 1, 0)
            store_block(NB - 2, 1, NB - 1)
            store_block(NB - 1, 0, NB)
            sp.wait_ge(o_stored[0], 16 * (NB // 2 + 1))
            sp.wait_ge(o_stored[1], 16 * (NB // 2))

        @block.gpsimd
        def _(pool):
            pool.memset(cleared, 0.0).then_inc(pool_step, 1)
            pool.memset(ident[:, :], 0.0).then_inc(pool_step, 1)
            pool.memset(ones[:, :], 1.0).then_inc(pool_step, 1)
            pool.memset(ones_cols[:, :], 1.0)
            pool.memset(eps_t[:, :], EPS)
            pool.memset(pos_f[:, :], 0.0).then_inc(pool_step, 1)
            pool.wait_ge(pool_step, 3)
            pool.memset(cleared[:, :, 2 * ED:2 * ED + 1], -1.0).then_inc(cleared_made, 2)
            pool.affine_select(out=ident[:, :], in_=ident[:, :], compare_op=ALU.not_equal, fill=1.0, base=0,
                               pattern=[[-1, P]], channel_multiplier=1)
            pool.affine_select(out=below[:, :], in_=ones[:, :], compare_op=ALU.is_gt, fill=0.0, base=0,
                               pattern=[[1, P]], channel_multiplier=-1)
            pool.iota(iota_i[:, :], pattern=[[1, NT]], base=0, channel_multiplier=0).then_inc(consts_ready, 1)
            pool.wait_ge(pool_step, 4)
            for b in range(BINS):
                pool.wait_ge(hit_ready, b + 1)
                if b:
                    pool.wait_ge(hit_added, b)
                pool.tensor_tensor(pos_f[:, :], pos_f[:, :], hit[:, b % 2, :], ALU.add).then_inc(hit_added, 1)

            def scatter(r, n):
                for c in range(n):
                    pool.indirect_dma_start(
                        out=sorted_rows, out_offset=bass.IndirectOffsetOnAxis(ap=slot_i[:, r, c:c + 1], axis=0),
                        in_=rows[:, r, c, :], in_offset=None).then_inc(scattered[r], 16)

            pool.wait_ge(slots_cleared, 16)
            with pool.Fori(0, FULL // 2) as it:
                for r in range(2):
                    pool.wait_ge(rows_built, 2 * it + (r + 1))
                    pool.sem_inc(pool_waited, 1)
                    scatter(r, CH)
            pool.wait_ge(rows_built, FULL + 1)
            scatter(0, CH_LAST)

            pool.memset(m_t[:, :, H:H + 1], 1.0)
            pool.memset(m_t[:, :, H + 1:SW], 0.0).then_inc(m_init, 1)
            pool.wait_ge(q_stored, 16 * NB)

            def gather(turn, j):
                t = turn * UN + j
                g = j // GRP
                if j % GRP == 0:
                    pool.wait_ge(srt_loaded[g], 16 * turn + 16)
                if not (isinstance(turn, int) and t < NG):
                    pool.wait_ge(pre_ready, t - (NG - 1))
                if not isinstance(turn, int):
                    pool.sem_inc(pool_waited, 1)
                at = (j % GRP) * ROW + ROW - 1
                pool.indirect_dma_start(
                    out=gath[:, j % NG, :], out_offset=None, in_=q_table,
                    in_offset=bass.IndirectOffsetOnAxis(ap=srt[:, g, at:at + 1].bitcast(I32), axis=0),
                ).then_inc(gathered[j % NG], 16)

            for j in range(UN):
                gather(0, j)
            with pool.Fori(1, NT // UN) as turn:
                for j in range(UN):
                    gather(turn, j)

            pool.wait_ge(s_added, NT)

            def copy_sums(b, r, free):
                if free is not None:
                    pool.wait_ge(sT_psum, free)
                pool.tensor_copy(s_in[:, r, :], xs[:, bass.ds(b * SW, SW)]).then_inc(s_copied, 1)

            def finish(b1_, r, stored):
                pool.wait_ge(zd_ready, b1_)
                if stored is not None:
                    pool.wait_ge(o_stored[r], stored)
                pool.tensor_tensor(upd[:, r, :], upd[:, r, :], nn[:, r, :], ALU.add).then_inc(pool_step, 1)
                pool.wait_ge(pool_step, b1_ + 4)
                pool.tensor_tensor(o_t[:, r, :], upd[:, r, :], x_in[:, r, :], ALU.add).then_inc(o_ready, 1)

            copy_sums(0, 0, None)
            copy_sums(1, 1, None)
            finish(1, 0, None)
            copy_sums(2, 0, 1)
            finish(2, 1, None)
            copy_sums(3, 1, 2)
            with pool.Fori(1, NB // 2 - 1) as it:
                for r in range(2):
                    finish(2 * it + (r + 1), r, 16 * it)
                    copy_sums(2 * it + (r + 2), r, 2 * it + (r + 1))
            finish(NB - 2, 0, 16 * (NB // 2 - 1))
            copy_sums(NB - 1, 0, NB - 2)
            finish(NB - 1, 1, 16 * (NB // 2 - 1))
            finish(NB, 0, 16 * (NB // 2))

        @block.vector
        def _(dve):
            n_step = [0]

            def link(ins):
                n_step[0] += 1
                ins.then_inc(dve_step, 1)
                dve.wait_ge(dve_step, n_step[0])

            V = nc.vector
            dve.wait_ge(src_in, 16)
            link(V.tensor_scalar(tmp_i[:, :], src_i[:, :], 7, None, ALU.arith_shift_right))
            link(V.tensor_copy(bin_f[:, :], tmp_i[:, :]))
            for b in range(BINS):
                V.tensor_scalar(mask[:, b * EC:(b + 1) * EC], bin_f[:, :], float(b), None, ALU.is_equal, ALU.add,
                                accum_out=counts[:, b:b + 1]).then_inc(counted, 1)
            V.tensor_scalar(tmp_i[:, :], src_i[:, :], P - 1, None, ALU.bitwise_and).then_inc(dve_step, 1)
            n_step[0] += 1
            dve.wait_ge(x_loaded, 16)
            for b in range(NB):
                V.bn_stats(stats[:, b, :], x_blk[:, b * H:(b + 1) * H])
            dve.wait_ge(dve_step, n_step[0])
            link(V.tensor_copy(loc_f[:, :], tmp_i[:, :]))
            dve.wait_ge(summed, 1)
            link(V.tensor_scalar(tiles_i[:, :], bank[0][:, 0:BINS], float(P - 1), None, ALU.add))
            link(V.tensor_scalar(tiles_i[:, :], tiles_i[:, :], 7, None, ALU.arith_shift_right))
            link(V.tensor_copy(tiles_f[:, :], tiles_i[:, :]))
            dve.wait_ge(consts_ready, 1)
            link(V.tensor_tensor_scan(tiles_end[:, :], ones[:, 0:BINS], tiles_f[:, :], 0.0, ALU.mult, ALU.add))
            link(V.tensor_tensor(tile_start[:, :], tiles_end[:, :], tiles_f[:, :], ALU.subtract))
            link(V.memset(tile_start[:, NB:BINS], float(NT)))
            link(V.tensor_scalar(base[:, :], tile_start[:, :], float(P), -1.0, ALU.mult, ALU.add))
            link(V.tensor_tensor(base[:, :], base[:, :], bank[0][:, 64:64 + BINS], ALU.add))
            for b in range(BINS):
                mb = mask[:, b * EC:(b + 1) * EC]
                V.tensor_tensor_scan(ranked[:, b % 2, :], ones_cols[:, :], mb, base[:, b:b + 1],
                                     ALU.mult, ALU.add).then_inc(dve_step, 1)
                n_step[0] += 1
                dve.wait_ge(dve_step, n_step[0])
                if b >= 2:
                    dve.wait_ge(hit_added, b - 1)
                V.tensor_tensor(hit[:, b % 2, :], ranked[:, b % 2, :], mb, ALU.mult).then_inc(hit_ready, 1)
            dve.wait_ge(hit_added, BINS)
            link(V.tensor_copy(pos_i[:, :], pos_f[:, :]))
            for b in range(NB):
                last = V.bn_aggr(mv[:, b, :], stats[:, b:b + 1, :])
            last.then_inc(var_ready, 1)
            dve.wait_ge(w_loaded, 16 * N_W)
            link(V.tensor_copy(w1c_hi[:, :], w1c_s[:, :]))
            V.tensor_tensor(w1c_lo[:, :], w1c_s[:, :], w1c_hi[:, :].bitcast(F32), ALU.subtract).then_inc(w1c_ready, 1)
            V.tensor_copy(iota_f[:, :], iota_i[:, :])
            dve.wait_ge(std_ready, 1)
            link(V.reciprocal(rstd[:, :], rstd[:, :]))
            V.scalar_tensor_tensor(out=nmr[:, :], in0=mv[:, :, 0], scalar=-1.0, in1=rstd[:, :],
                                   op0=ALU.mult, op1=ALU.mult).then_inc(norm_ready, 1)
            for c in range(2):
                dve.wait_ge(wc_psum, c + 1)
                V.tensor_copy(wc_s[:, c, 0:512], bank[1 + 2 * c][:, :])
                V.tensor_copy(wc_s[:, c, 512:G3], bank[2 + 2 * c][:, 0:256])
            dve.wait_ge(wc_psum, 3)
            V.tensor_copy(cb_s[0:1, 0:512], bank[5][0:1, :])
            V.tensor_copy(cb_s[0:1, 512:G3], bank[6][0:1, 0:256]).then_inc(wc_ready, 1)
            dve.wait_ge(dst_in, 16)

            def build(k, r, n, turn, k1):
                if turn is not None:
                    dve.wait_ge(scattered[r], SCAT * turn)
                col = k * CH
                V.tensor_copy(rows[:, r, 0:n, 2 * ED], loc_f[:, bass.ds(col, n)])
                V.tensor_copy(rows[:, r, 0:n, 2 * ED + 1].bitcast(I32), dst_i[:, bass.ds(col, n)])
                V.tensor_copy(slot_i[:, r, 0:n], pos_i[:, bass.ds(col, n)])
                dve.wait_ge(hi_built, k1)
                V.tensor_tensor(rows[:, r, 0:n, ED:2 * ED], ea_in[:, r, 0:n, :], rows[:, r, 0:n, 0:ED],
                                ALU.subtract).then_inc(rows_built, 1)

            def node_block(b, b1_, first):
                dve.wait_ge(pq_psum, b1_)
                if not first:
                    dve.wait_ge(p_done, b1_ - 1)
                V.tensor_tensor(p_tmp[:, :], bank[1][:, 0:H], b1_s[:, :], ALU.add).then_inc(p_ready, 1)
                dve.wait_ge(gh_psum, b1_)
                V.tensor_tensor(g_tmp[:, 0:512], bank[2][:, :], bhh_s[:, 0:512], ALU.add)
                V.tensor_tensor(g_tmp[:, 512:G3], bank[3][:, 0:256], bhh_s[:, 512:G3], ALU.add).then_inc(gh_ready, 1)
                dve.wait_ge(p_hi, b1_)
                hi = p_tab[:, bass.ds(b * (2 * H), H)]
                V.tensor_tensor(p_tab[:, bass.ds(b * (2 * H) + H, H)], p_tmp[:, :], hi.bitcast(F32),
                                ALU.subtract).then_inc(p_done, 1)

            build(0, 0, CH, None, 1)
            build(1, 1, CH, None, 2)
            node_block(0, 1, True)
            node_block(1, 2, False)
            with dve.Fori(1, FULL // 2) as it:
                for r in range(2):
                    build(2 * it + r, r, CH, it, 2 * it + (r + 1))
                    node_block(2 * it + r, 2 * it + (r + 1), False)
            build(FULL, 0, CH_LAST, FULL // 2, FULL + 1)
            node_block(FULL, FULL + 1, False)

            dve.wait_ge(h_ready, NB)
            link(V.memset(xs[:, :], 0.0))
            link(V.memset(xs[:, :].rearrange("p (b w) -> p b w", w=SW)[:, :, SW - 1:SW], 1.0))
            link(V.tensor_scalar(blk_f[:, :], iota_f[0:1, :], tile_start[0:1, 1:2], None, ALU.is_ge))
            for b in range(2, NB):
                link(V.scalar_tensor_tensor(out=blk_f[:, :], in0=iota_f[0:1, :], scalar=tile_start[0:1, b:b + 1],
                                            in1=blk_f[:, :], op0=ALU.is_ge, op1=ALU.add))
            V.tensor_scalar(off_p[:, :], blk_f[:, :], float(2 * H), None, ALU.mult)
            link(V.tensor_scalar(off_s[:, :], blk_f[:, :], float(SW), None, ALU.mult))
            dve.sem_inc(tabs_ready, 1)

            def one_hot(turn, j):
                g = j // GRP
                if j % GRP == 0:
                    dve.wait_ge(srt_loaded[g], 16 * turn + 16)
                at = (j % GRP) * ROW + ROW - 2
                V.tensor_scalar(oh[:, j % 8, :], iota_f[:, 0:P], srt[:, g, at:at + 1], None, ALU.is_equal
                                ).then_inc(oh_ready, 1)

            def terms(turn, j):
                t = turn * UN + j
                dve.wait_ge(pre_psum, t + 1)
                dve.wait_ge(gathered[j % NG], (32 * turn) + 16 * (j // NG + 1))
                if not (isinstance(t, int) and t < 4):
                    dve.wait_ge(m_ready, t - 3)
                V.tensor_tensor(pre[:, j % 4, :], ps_pre[j % 4][:, 0:H], gath[:, j % NG, :], ALU.add
                                ).then_inc(pre_ready, 1)

            def add_sums(turn, j, off):
                t = turn * UN + j
                dve.wait_ge(seg_psum, t + 1)
                if not (isinstance(t, int) and t < 1):
                    dve.wait_ge(s_added, t)
                s = xs[:, bass.ds(off, SW)]
                V.tensor_tensor(s, s, ps_seg[j % 2][:, 0:SW], ALU.add).then_inc(s_added, 1)

            def offsets(turn, eng_type, tab, top):
                _, vals = nc.values_load_multi_w_load_instructions(
                    tab[0:1, bass.ds(turn * UN, UN)], engines=[eng_type], min_val=0, max_val=top,
                    skip_runtime_bounds_check_because="a block number of 0..NB-1 by its own computation")
                return vals

            def turn_of(turn, first, last):
                if first:
                    for j in range(4):
                        one_hot(turn, j)
                    for j in range(2):
                        terms(turn, j)
                offs = offsets(turn, mybir.EngineType.DVE, off_s, (NB - 1) * SW)
                for j in range(UN):
                    if not last or j + 4 < UN:
                        one_hot(turn + (j + 4) // UN, (j + 4) % UN)
                    if not last or j + 2 < UN:
                        terms(turn + (j + 2) // UN, (j + 2) % UN)
                    add_sums(turn, j, offs[j])

            turn_of(0, True, False)
            with dve.Fori(1, NT // UN - 1) as turn:
                turn_of(turn, False, False)
            turn_of(NT // UN - 1, False, True)

            def update(r, b1_, loads, d0):
                dve.wait_ge(gx_psum, b1_)
                dve.wait_ge(xg_loaded[r], loads)
                V.tensor_tensor(rz[:, r, :], bank[2 + r][:, :], g_in[:, r, 0:512], ALU.add).then_inc(rz_sum, 1)
                dve.wait_ge(rz_ready, b1_)
                V.tensor_tensor(nn[:, r, :], rz[:, r, 0:H], g_in[:, r, 512:G3], ALU.mult).then_inc(dve_step, 1)
                dve.wait_ge(dve_step, d0 + 1)
                V.tensor_tensor(nn[:, r, :], nn[:, r, :], bank[4 + r][:, 0:H], ALU.add).then_inc(n_sum, 1)
                dve.wait_ge(n_ready, b1_)
                V.tensor_tensor(upd[:, r, :], g_in[:, r, G3:GW], nn[:, r, :], ALU.subtract).then_inc(dve_step, 1)
                dve.wait_ge(dve_step, d0 + 2)
                V.tensor_tensor(upd[:, r, :], upd[:, r, :], rz[:, r, H:2 * H], ALU.mult).then_inc(zd_ready, 1)

            s0 = n_step[0]
            update(0, 1, 32, s0)
            update(1, 2, 32, s0 + 2)
            with dve.Fori(1, NB // 2) as it:
                for r in range(2):
                    update(r, 2 * it + (r + 1), 32 * it + 32, 4 * it + (s0 + 2 * r))
            update(0, NB, 32 * (NB // 2 + 1), s0 + 2 * (NB - 1))

        @block.scalar
        def _(act):
            A = nc.scalar
            act.wait_ge(consts_ready, 1)
            act.wait_ge(var_ready, 1)
            A.activation(rstd[:, :], mv[:, :, 1], ACT.Sqrt, bias=eps_t[:, :]).then_inc(std_ready, 1)

            def build(r, n, loads, turn):
                act.wait_ge(ea_loaded[r], loads)
                if turn is not None:
                    act.wait_ge(scattered[r], SCAT * turn)
                A.activation(rows[:, r, 0:n, 0:ED].bitcast(F32R), ea_in[:, r, 0:n, :], ACT.Copy
                             ).then_inc(hi_built, 1)

            def node_block(b, b1_, first):
                if not first:
                    act.wait_ge(g_stored, 16 * (b1_ - 1))
                A.activation(g_tmp[:, G3:GW], xs[:, bass.ds(b * H, H)], ACT.Relu, bias=nmr[:, bass.ds(b, 1)],
                             scale=rstd[:, bass.ds(b, 1)]).then_inc(h_ready, 1)
                act.wait_ge(hT_psum, b1_)
                A.activation(hT[:, :, :], bank[0][:, 0:2 * P].rearrange("p (a b) -> p a b", a=2), ACT.Copy
                             ).then_inc(hT_ready, 1)
                act.wait_ge(pq_psum, b1_)
                if not first:
                    act.wait_ge(q_stored, 16 * (b1_ - 1))
                A.activation(q_tmp[:, :], bank[4][:, 0:H], ACT.Copy).then_inc(q_ready, 1)
                act.wait_ge(p_ready, b1_)
                A.activation(p_tab[:, bass.ds(b * (2 * H), H)], p_tmp[:, :], ACT.Copy).then_inc(p_hi, 1)
                act.wait_ge(q_ready, b1_)
                act.dma_start(q_v[:, bass.ds(b, 1), :].rearrange("p b f -> p (b f)"), q_tmp[:, :]
                              ).then_inc(q_stored, 16)
                act.wait_ge(gh_ready, b1_)
                act.wait_ge(h_ready, b1_)
                act.dma_start(spill_v[:, bass.ds(b, 1), :].rearrange("p b f -> p (b f)"), g_tmp[:, :]
                              ).then_inc(g_stored, 16)

            build(0, CH, 16, None)
            build(1, CH, 16, None)
            act.wait_ge(norm_ready, 1)
            node_block(0, 1, True)
            node_block(1, 2, False)
            with act.Fori(1, FULL // 2) as it:
                for r in range(2):
                    build(r, CH, 16 * it + 16, it)
                    node_block(2 * it + r, 2 * it + (r + 1), False)
            build(0, CH_LAST, 16 * (FULL // 2 + 1), FULL // 2)
            node_block(FULL, FULL + 1, False)
            act.wait_ge(m_init, 1)

            def copy_transposed(turn, j):
                act.wait_ge(tr_psum, turn * UN + (j + 1))
                A.activation(tT[:, j % 4, :], ps_tr[j % 2][:, 0:2 * P], ACT.Copy).then_inc(tT_ready, 1)

            def relu(turn, j):
                t = turn * UN + j
                act.wait_ge(pre_ready, t + 1)
                if not (isinstance(t, int) and t < 4):
                    act.wait_ge(seg_psum, t - 3)
                A.activation(m_t[:, j % 4, 0:H], pre[:, j % 4, :], ACT.Relu).then_inc(m_ready, 1)

            def turn_of(turn, first, last):
                if first:
                    for j in range(3):
                        copy_transposed(turn, j)
                    for j in range(2):
                        relu(turn, j)
                for j in range(UN):
                    if not last or j + 3 < UN:
                        copy_transposed(turn + (j + 3) // UN, (j + 3) % UN)
                    if not last or j + 2 < UN:
                        relu(turn + (j + 2) // UN, (j + 2) % UN)

            turn_of(0, True, False)
            with act.Fori(1, NT // UN - 1) as turn:
                turn_of(turn, False, False)
            turn_of(NT // UN - 1, False, True)

            def sums_T(r, b1_):
                act.wait_ge(sT_psum, b1_)
                A.activation(sT[:, r, :], bank[r][:, 0:2 * P], ACT.Copy)
                A.activation(cT[0:2, r, :], bank[r][0:2, 2 * P:3 * P], ACT.Copy).then_inc(sT_ready, 1)

            def gates(r, b1_):
                act.wait_ge(rz_sum, b1_)
                A.activation(rz[:, r, :], rz[:, r, :], ACT.Sigmoid).then_inc(rz_ready, 1)
                act.wait_ge(n_sum, b1_)
                A.activation(nn[:, r, :], nn[:, r, :], ACT.Tanh).then_inc(n_ready, 1)

            sums_T(0, 1)
            with act.Fori(0, NB // 2) as it:
                sums_T(1, 2 * it + 2)
                gates(0, 2 * it + 1)
                sums_T(0, 2 * it + 3)
                gates(1, 2 * it + 2)
            gates(0, NB)

        @block.tensor
        def _(pe):
            T = nc.tensor
            pe.wait_ge(consts_ready, 1)
            pe.wait_ge(counted, BINS)
            T.matmul(bank[0][:, 0:BINS], ones[:, :], counts[:, :], start=True, stop=True)
            T.matmul(bank[0][:, 64:64 + BINS], below[:, :], counts[:, :], start=True, stop=True).then_inc(summed, 1)
            pe.wait_ge(w_loaded, 16 * N_W)
            for k in range(2):
                for lo, n, bk in ((0, 512, bank[1 + 2 * k]), (512, 256, bank[2 + 2 * k])):
                    for c in range(2):
                        last = T.matmul(bk[:, 0:n], w2_s[:, c, k * P:(k + 1) * P], wih_s[:, c, lo:lo + n],
                                        start=(c == 0), stop=(c == 1))
                last.then_inc(wc_psum, 1)
            for lo, n, bk in ((0, 512, bank[5]), (512, 256, bank[6])):
                for c in range(2):
                    last = T.matmul(bk[0:1, 0:n], b2_s[:, c:c + 1], wih_s[:, c, lo:lo + n],
                                    start=(c == 0), stop=(c == 1))
            last.then_inc(wc_psum, 1)
            pe.wait_ge(wc_ready, 1)

            def node_block(b1_, first):
                pe.wait_ge(h_ready, b1_)
                for c in range(2):
                    last = T.transpose(bank[0][:, c * P:(c + 1) * P], g_tmp[:, G3 + c * P:G3 + (c + 1) * P], ident[:, :])
                last.then_inc(hT_psum, 1)
                pe.wait_ge(hT_ready, b1_)
                if not first:
                    pe.wait_ge(q_ready, b1_ - 1)
                    pe.wait_ge(p_ready, b1_ - 1)
                for lo, bk in ((0, bank[1]), (H, bank[4])):
                    for c in range(2):
                        last = T.matmul(bk[:, 0:H], hT[:, c, :], w1pq_s[:, c, lo:lo + H],
                                        start=(c == 0), stop=(c == 1))
                last.then_inc(pq_psum, 1)
                if not first:
                    pe.wait_ge(gh_ready, b1_ - 1)
                for lo, n, bk in ((0, 512, bank[2]), (512, 256, bank[3])):
                    for c in range(2):
                        last = T.matmul(bk[:, 0:n], hT[:, c, :], whh_s[:, c, lo:lo + n],
                                        start=(c == 0), stop=(c == 1))
                last.then_inc(gh_psum, 1)

            node_block(1, True)
            with pe.Fori(2, NB + 1) as b1_:
                node_block(b1_, False)

            pe.wait_ge(tabs_ready, 1)
            pe.wait_ge(p_done, NB)
            pe.wait_ge(gh_ready, NB)
            pe.wait_ge(w1c_ready, 1)

            def transposes(turn, j):
                t = turn * UN + j
                pe.wait_ge(oh_ready, t + 1)
                if not (isinstance(t, int) and t < 2):
                    pe.wait_ge(tT_ready, t - 1)
                g, at = j // GRP, (j % GRP) * ROW
                T.transpose(ps_tr[j % 2][:, 0:P], srt[:, g, at:at + P], ident[:, :])
                T.transpose(ps_tr[j % 2][:, P:2 * P], oh[:, j % 8, :], ident[:, :]).then_inc(tr_psum, 1)

            def terms(turn, j, off):
                t = turn * UN + j
                pe.wait_ge(tT_ready, t + 1)
                if not (isinstance(t, int) and t < 4):
                    pe.wait_ge(pre_ready, t - 3)
                acc = ps_pre[j % 4][:, 0:H]
                T.matmul(acc, tT[:, j % 4, 0:P], w1c_hi[:, :], start=True, stop=False)
                T.matmul(acc, tT[:, j % 4, 0:P], w1c_lo[:, :], start=False, stop=False)
                T.matmul(acc, tT[:, j % 4, P:2 * P], p_tab[:, bass.ds(off, H)], start=False, stop=False)
                T.matmul(acc, tT[:, j % 4, P:2 * P], p_tab[:, bass.ds(off + H, H)], start=False, stop=True
                         ).then_inc(pre_psum, 1)

            def node_sums(turn, j):
                t = turn * UN + j
                pe.wait_ge(m_ready, t + 1)
                if not (isinstance(t, int) and t < 2):
                    pe.wait_ge(s_added, t - 1)
                T.matmul(ps_seg[j % 2][:, 0:SW], oh[:, j % 8, :], m_t[:, j % 4, :], start=True, stop=True
                         ).then_inc(seg_psum, 1)

            def offsets(turn):
                _, vals = nc.values_load_multi_w_load_instructions(
                    off_p[0:1, bass.ds(turn * UN + 2, UN) if not isinstance(turn, int) or turn * UN + 2 + UN <= NT
                          else slice(turn * UN + 2, NT)],
                    engines=[mybir.EngineType.PE], min_val=0, max_val=(NB - 1) * 2 * H,
                    skip_runtime_bounds_check_because="a block number of 0..NB-1 by its own computation")
                return vals

            def turn_of(turn, first, last):
                if first:
                    _, head = nc.values_load_multi_w_load_instructions(
                        off_p[0:1, 0:2], engines=[mybir.EngineType.PE], min_val=0, max_val=(NB - 1) * 2 * H,
                        skip_runtime_bounds_check_because="a block number of 0..NB-1 by its own computation")
                    for j in range(3):
                        transposes(turn, j)
                        if j < 2:
                            terms(turn, j, head[j])
                offs = offsets(turn)
                for j in range(UN):
                    if not last or j + 3 < UN:
                        transposes(turn + (j + 3) // UN, (j + 3) % UN)
                    if not last or j + 2 < UN:
                        terms(turn + (j + 2) // UN, (j + 2) % UN, offs[j])
                    node_sums(turn, j)

            turn_of(0, True, False)
            with pe.Fori(1, NT // UN - 1) as turn:
                turn_of(turn, False, False)
            turn_of(NT // UN - 1, False, True)

            pe.wait_ge(s_added, NT)

            def sums_T(r, b1_, free):
                pe.wait_ge(s_copied, b1_)
                if free is not None:
                    pe.wait_ge(sT_ready, free)
                for c in range(2):
                    T.transpose(bank[r][:, c * P:(c + 1) * P], s_in[:, r, c * P:(c + 1) * P], ident[:, :])
                T.transpose(bank[r][0:2, 2 * P:3 * P], s_in[:, r, H:SW], ident[:, :]).then_inc(sT_psum, 1)

            def gates(r, b1_, free):
                pe.wait_ge(sT_ready, b1_)
                if free is not None:
                    pe.wait_ge(n_sum, free)
                for lo, n, bk in ((0, 512, bank[2 + r]), (512, 256, bank[4 + r])):
                    for c in range(2):
                        T.matmul(bk[:, 0:n], sT[:, r, c * P:(c + 1) * P], wc_s[:, c, lo:lo + n],
                                 start=(c == 0), stop=False)
                    last = T.matmul(bk[:, 0:n], cT[0:2, r, :], cb_s[:, lo:lo + n], start=False, stop=True)
                last.then_inc(gx_psum, 1)

            sums_T(0, 1, None)
            sums_T(1, 2, None)
            gates(0, 1, None)
            sums_T(0, 3, 1)
            gates(1, 2, None)
            with pe.Fori(1, NB // 2) as it:
                sums_T(1, 2 * it + 2, 2 * it)
                gates(0, 2 * it + 1, 2 * it - 1)
                sums_T(0, 2 * it + 3, 2 * it + 1)
                gates(1, 2 * it + 2, 2 * it)
            gates(0, NB, NB - 2)


def kernel(x, src, dst, edge_attr_64, L0_gnn_W1, L0_gnn_b1, L0_gnn_W2, L0_gnn_b2, L0_gnn_W_ih, L0_gnn_b_ih,
           L0_gnn_W_hh, L0_gnn_b_hh):
    import numpy as np
    import concourse.bacc as bacc
    from concourse.bass_utils import run_bass_kernel_spmd

    w1 = np.asarray(L0_gnn_W1)
    pad_n, pad_e = NODES_PAD - NODES, EDGES_PAD - EDGES
    arrays = {
        "x": np.pad(np.asarray(x), ((0, pad_n), (0, 0))),
        "src": np.pad(np.asarray(src), (0, pad_e), constant_values=NODES_PAD),
        "dst": np.pad(np.asarray(dst), (0, pad_e)),
        "ea": np.pad(np.asarray(edge_attr_64), ((0, pad_e), (0, 0))),
        "w1pq": np.concatenate([w1[:, 0:H].T, w1[:, H:2 * H].T], axis=1),
        "w1c": w1[:, 2 * H:].T,
        "w2": np.asarray(L0_gnn_W2),
        "wih": np.asarray(L0_gnn_W_ih).T,
        "whh": np.asarray(L0_gnn_W_hh).T,
        "b1": np.asarray(L0_gnn_b1), "b2": np.asarray(L0_gnn_b2),
        "bih": np.asarray(L0_gnn_b_ih), "bhh": np.asarray(L0_gnn_b_hh),
    }
    arrays = {k: np.ascontiguousarray(v) for k, v in arrays.items()}
    nc = bacc.Bacc("TRN2", target_bir_lowering=False, num_devices=1)
    args = [nc.dram_tensor(f"in_{k}", v.shape, mybir.dt.from_np(v.dtype), kind="ExternalInput").ap()
            for k, v in arrays.items()]
    out = nc.dram_tensor("out", (NODES_PAD, H), F32, kind="ExternalOutput").ap()
    gnn_layer(nc, *args, out)
    r = run_bass_kernel_spmd(nc, [{f"in_{k}": v for k, v in arrays.items()}], core_ids=[0])
    return r.results[0]["out"][0:NODES]
```

```python
import concourse.bass as bass
from concourse import mybir
from contextlib import ExitStack

F32 = mybir.dt.float32
F32R = mybir.dt.float32r
BF16 = mybir.dt.bfloat16
I32 = mybir.dt.int32
ALU = mybir.AluOpType
ACT = mybir.ActivationFunctionType

P = 128
NODES, EDGES, H, ED = 3125, 50000, 256, 64
G3 = 3 * H
NB = -(-NODES // P)
NODES_PAD = NB * P
EC = -(-EDGES // P)
EDGES_PAD = EC * P
BINS = NB + 1
CH = 16
FULL = EC // CH
CH_LAST = EC - FULL * CH
UN = 16
NT = -(-((EDGES + NB * (P - 1)) // P) // UN) * UN
SLOTS = NT * P
GRP = 4
NGRP = UN // GRP
NG = 16
ROW = 2 * ED + 2
SW = H + 1
CX = 6
GW = G3 + H
EPS = 1e-5
UB = 6
assert FULL == NB - 1 and FULL % 2 == 0 and NB % UB == 1 and NG == UN


def gnn_layer(nc, x, src, dst, ea, w1pq, w1c, w2, wih, whh, b1, b2, bih, bhh, out):
    ctx = ExitStack()
    with ctx:
        def sb(name, shape, dt=F32):
            return ctx.enter_context(nc.sbuf_tensor(name, shape, dt))

        def sem(name):
            return ctx.enter_context(nc.semaphore(name))

        sorted_rows = nc.dram_tensor("sorted_rows", [SLOTS + P, ROW], F32, kind="Internal").ap()
        q_table = nc.dram_tensor("q_table", [NODES_PAD, H], F32, kind="Internal").ap()
        spill = nc.dram_tensor("spill", [NODES_PAD, GW], F32, kind="Internal").ap()

        ident = sb("ident", [P, P])
        ones = sb("ones", [P, P])
        below = sb("below", [P, P])
        zeros = sb("zeros", [P, SW])
        empty_row = sb("empty_row", [P, ROW])
        iota_i = sb("iota_i", [P, NT], I32)
        iota_f = sb("iota_f", [P, NT])
        eps_t = sb("eps_t", [P, 1])
        w1pq_s = sb("w1pq_s", [P, 2, 2 * H])
        w1c_s = sb("w1c_s", [P, H])
        w1c_hi = sb("w1c_hi", [P, H], F32R)
        w1c_lo = sb("w1c_lo", [P, H], F32R)
        w2_s = sb("w2_s", [P, 2, H])
        wih_s = sb("wih_s", [P, 2, G3])
        whh_s = sb("whh_s", [P, 2, G3])
        wc_s = sb("wc_s", [P, 2, G3])
        cb_s = sb("cb_s", [CX, G3], F32R)
        b1_s = sb("b1_s", [P, H])
        bhh_s = sb("bhh_s", [P, G3])
        b2_s = sb("b2_s", [P, 2])

        src_i = sb("src_i", [P, EC], I32)
        dst_i = sb("dst_i", [P, EC], I32)
        tmp_i = sb("tmp_i", [P, EC], I32)
        bin_f = sb("bin_f", [P, (FULL + 1) * CH])
        loc_f = sb("loc_f", [P, EC])
        junk = sb("junk", [P, 2, EC], BF16)
        in_bin = sb("in_bin", [P, BINS, CH])
        ranked = sb("ranked", [P, 2, BINS, CH])
        picked = sb("picked", [P, BINS, CH])
        slot_f = sb("slot_f", [P, 2, CH])
        counts = sb("counts", [P, BINS])
        tiles_i = sb("tiles_i", [P, BINS], I32)
        tiles_f = sb("tiles_f", [P, BINS])
        tiles_end = sb("tiles_end", [P, BINS])
        tile_start = sb("tile_start", [P, BINS])
        base = sb("base", [P, BINS])
        last_tile = sb("last_tile", [1, NB], I32)
        blk_f = sb("blk_f", [1, NT])
        off_p = sb("off_p", [1, NT], I32)
        off_s = sb("off_s", [1, NT], I32)

        xs = sb("xs", [P, NB * SW])
        xs_b = xs[:, :].rearrange("p (b w) -> p b w", w=SW)
        stats = sb("stats", [P, NB, 6])
        mv = sb("mv", [P, NB, 2])
        rstd = sb("rstd", [P, NB])
        nmr = sb("nmr", [P, NB])

        p_tab = sb("p_tab", [P, NB * 2 * H], F32R)
        hT = sb("hT", [P, 2, P])
        p_tmp = sb("p_tmp", [P, H])
        q_tmp = sb("q_tmp", [P, H])
        g_tmp = sb("g_tmp", [P, GW])
        slot_i = sb("slot_i", [P, 2, CH], I32)

        oh = sb("oh", [P, 8, P])
        tT = sb("tT", [P, 4, 2 * P], F32R)
        cnt_x = sb("cnt_x", [P, NB, CX])
        arena = sb("arena", [P, 9280])

        def cut(at, *dims):
            n = 1
            for d in dims:
                n *= d
            names = " ".join("abc"[:len(dims)])
            v = arena[:, at:at + n]
            return v if len(dims) == 1 else v.rearrange(
                f"p ({names}) -> p {names}", **{c: d for c, d in zip("abc", dims)})

        rows = cut(0, 2, CH, ROW)
        ea_in = cut(4160, 2, CH, ED)
        cwb = cut(6208, 4, G3)
        srt = cut(0, NGRP, GRP * ROW)
        gath = cut(2080, NG, H)
        m_t = cut(6208, 4, SW)
        pre = cut(7240, 4, H)
        x_in = cut(0, 3, H)
        g_in = cut(768, 3, GW)
        s_in = cut(3840, 2, H + CX)
        sT = cut(4368, 2, H)
        rz = cut(4880, 3, 2 * H)
        nn = cut(6416, 3, H)
        upd = cut(7184, 3, H)
        o_t = cut(7952, 3, H)
        cT = sb("cT", [CX, 2, P], F32R)
        bih_s = sb("bih_s", [1, G3])
        cw_s = sb("cw_s", [1, G3])

        bank = [ctx.enter_context(nc.psum_tensor(f"bank{i}", [P, 512], F32)) for i in range(8)]
        ps_tr, ps_pre, ps_seg = bank[0:2], bank[2:6], bank[6:8]
        ps_rz, ps_n = bank[2:5], bank[5:8]

        src_in, dst_in, x_loaded = sem("src_in"), sem("dst_in"), sem("x_loaded")
        w_loaded = sem("w_loaded")
        empty_made, last_tiles = sem("empty_made"), sem("last_tiles")
        spare_cleared, slots_cleared = sem("spare_cleared"), sem("slots_cleared")
        pool_step, dve_step, act_step = sem("pool_step"), sem("dve_step"), sem("act_step")
        consts_ready = sem("consts_ready")
        pool_waited = sem("pool_waited")
        counted, summed = sem("counted"), sem("summed")
        place_step, slots_ready = sem("place_step"), sem("slots_ready")
        var_ready, std_ready, norm_ready = sem("var_ready"), sem("std_ready"), sem("norm_ready")
        wc_psum, wc_ready = sem("wc_psum"), sem("wc_ready")
        w1c_ready = sem("w1c_ready")
        cb_cut, cb_moved = sem("cb_cut"), sem("cb_moved")
        ea_loaded = [sem(f"ea_loaded{r}") for r in range(2)]
        hi_built, rows_built = sem("hi_built"), sem("rows_built")
        scattered = [sem(f"scattered{r}") for r in range(2)]
        h_ready, hT_psum, hT_ready = sem("h_ready"), sem("hT_psum"), sem("hT_ready")
        pq_psum, gh_psum = sem("pq_psum"), sem("gh_psum")
        p_ready, p_hi, p_done = sem("p_ready"), sem("p_hi"), sem("p_done")
        q_ready, gh_ready = sem("q_ready"), sem("gh_ready")
        q_stored, g_stored = sem("q_stored"), sem("g_stored")
        tabs_ready = sem("tabs_ready")
        m_init = sem("m_init")
        srt_loaded = [sem(f"srt_loaded{g}") for g in range(NGRP)]
        gathered = [sem(f"gathered{g}") for g in range(NG)]
        oh_ready, tr_psum, tT_ready = sem("oh_ready"), sem("tr_psum"), sem("tT_ready")
        pre_psum, pre_ready, m_ready = sem("pre_psum"), sem("pre_ready"), sem("m_ready")
        seg_psum, s_added = sem("seg_psum"), sem("s_added")
        xg_loaded = [sem(f"xg_loaded{r}") for r in range(3)]
        cnt_ready = sem("cnt_ready")
        s_copied, sT_psum, sT_ready = sem("s_copied"), sem("sT_psum"), sem("sT_ready")
        gx_psum, rz_sum, rz_ready = sem("gx_psum"), sem("rz_sum"), sem("rz_ready")
        rn_ready, n_sum, n_ready = sem("rn_ready"), sem("n_sum"), sem("n_ready")
        hn_ready, zd_ready, nzd_ready = sem("hn_ready"), sem("zd_ready"), sem("nzd_ready")
        o_ready = sem("o_ready")
        o_stored = [sem(f"o_stored{r}") for r in range(3)]

        block = ctx.enter_context(nc.Block())

        SCAT = 16 * CH
        ea_v = ea.rearrange("(p c) d -> p c d", p=P)
        sorted_v = sorted_rows[0:SLOTS, :].rearrange("(t p) c -> p t c", p=P)
        x_v = x.rearrange("(b p) f -> p b f", p=P)
        q_v = q_table.rearrange("(b p) f -> p b f", p=P)
        spill_v = spill.rearrange("(b p) f -> p b f", p=P)
        out_v = out.rearrange("(b p) f -> p b f", p=P)
        N_W = 11

        def is_int(v, low):
            return isinstance(v, int) and v < low

        @block.sync
        def _(sp):
            sp.dma_start(src_i[:, :], src.rearrange("(p c) -> p c", p=P)).then_inc(src_in, 16)
            sp.dma_start(dst_i[:, :], dst.rearrange("(p c) -> p c", p=P)).then_inc(dst_in, 16)
            for r in range(2):
                sp.dma_start(ea_in[:, r, :, :], ea_v[:, r * CH:(r + 1) * CH, :]).then_inc(ea_loaded[r], 16)
            sp.wait_ge(empty_made, 2)
            spare = EDGES_PAD // P
            sp.dma_start(sorted_v[:, spare:NT, :], empty_row[:, :].unsqueeze(1).to_broadcast([P, NT - spare, ROW])
                         ).then_inc(spare_cleared, 16)
            sp.dma_start(xs_b[:, :, 0:H], x_v).then_inc(x_loaded, 16)
            for tile_, view in (
                (w1pq_s[:, :, :], w1pq.rearrange("(c p) n -> p c n", p=P)),
                (w1c_s[0:ED, :], w1c), (w1c_s[ED:2 * ED, :], w1c),
                (w2_s[:, :, :], w2.rearrange("(c p) n -> p c n", p=P)),
                (wih_s[:, :, :], wih.rearrange("(c p) n -> p c n", p=P)),
                (whh_s[:, :, :], whh.rearrange("(c p) n -> p c n", p=P)),
                (b1_s[:, :], b1.rearrange("(a n) -> a n", a=1).to_broadcast([P, H])),
                (bhh_s[:, :], bhh.rearrange("(a n) -> a n", a=1).to_broadcast([P, G3])),
                (b2_s[:, 0:1], b2[0:P].rearrange("(p a) -> p a", a=1)),
                (b2_s[:, 1:2], b2[P:2 * P].rearrange("(p a) -> p a", a=1)),
                (bih_s[0:1, :], bih.rearrange("(a n) -> a n", a=1)),
            ):
                sp.dma_start(tile_, view).then_inc(w_loaded, 16)
            sp.wait_ge(last_tiles, 1)
            sp.wait_ge(spare_cleared, 16)
            _, last = nc.values_load_multi_w_load_instructions(
                last_tile[0:1, 0:NB], engines=[mybir.EngineType.SP], min_val=0, max_val=NT - 1,
                skip_runtime_bounds_check_because="a tile number of 0..NT-1 by its own computation")
            for b in range(NB):
                sp.dma_start(sorted_v[:, bass.ds(last[b], 1), :].rearrange("p t c -> p (t c)"), empty_row[:, :]
                             ).then_inc(slots_cleared, 16)
            sp.wait_ge(cb_cut, 1)
            for row, part in enumerate((0, 1, 0, 1, 2, 3)):
                sp.dma_start(cb_s[row:row + 1, :].bitcast(F32), cwb[0:1, part, :]).then_inc(cb_moved, 16)
            with sp.Fori(1, FULL // 2) as it:
                for r in range(2):
                    sp.wait_ge(rows_built, 2 * it + r - 1)
                    sp.dma_start(ea_in[:, r, :, :], ea_v[:, bass.ds(it * (2 * CH) + r * CH, CH), :]
                                 ).then_inc(ea_loaded[r], 16)
            sp.wait_ge(rows_built, FULL - 1)
            sp.dma_start(ea_in[:, 0, 0:CH_LAST, :], ea_v[:, FULL * CH:EC, :]).then_inc(ea_loaded[0], 16)

            sp.wait_ge(scattered[0], SCAT * (FULL // 2) + 16 * CH_LAST)
            sp.wait_ge(scattered[1], SCAT * (FULL // 2))

            def load_group(turn, g):
                sp.dma_start(srt[:, g, :].rearrange("p (t c) -> p t c", t=GRP),
                             sorted_v[:, bass.ds(turn * UN + g * GRP, GRP), :]).then_inc(srt_loaded[g], 16)

            for g in range(NGRP):
                load_group(0, g)
            with sp.Fori(1, NT // UN) as turn:
                for g in range(NGRP):
                    sp.wait_ge(pre_ready, turn * UN + (g + 1) * GRP - UN)
                    load_group(turn, g)

            sp.wait_ge(s_added, NT)
            sp.wait_ge(g_stored, 16 * NB)

            def load_block(b, r):
                sp.dma_start(x_in[:, r, :], x_v[:, bass.ds(b, 1), :].rearrange("p b f -> p (b f)")
                             ).then_inc(xg_loaded[r], 16)
                sp.dma_start(g_in[:, r, :], spill_v[:, bass.ds(b, 1), :].rearrange("p b f -> p (b f)")
                             ).then_inc(xg_loaded[r], 16)

            def store_block(b, j, last):
                sp.wait_ge(o_ready, b + 1)
                sp.dma_start(out_v[:, bass.ds(b, 1), :].rearrange("p b f -> p (b f)"), o_t[:, j % 3, :]
                             ).then_inc(o_stored[j % 3], 16)
                if not last:
                    load_block(b + 3, j % 3)

            for b in range(3):
                load_block(b, b)
            with sp.Fori(0, NB // UB - 1) as turn:
                for j in range(UB):
                    store_block(turn * UB + j, j, False)
            for b in range(NB - 1 - UB, NB):
                store_block(b, b % UB, b + 3 >= NB)
            for r in range(3):
                sp.wait_ge(o_stored[r], 16 * len(range(r, NB, 3)))

        @block.gpsimd
        def _(pool):
            pool.memset(empty_row[:, :], 0.0).then_inc(pool_step, 1)
            pool.memset(ident[:, :], 0.0).then_inc(pool_step, 1)
            pool.memset(ones[:, :], 1.0).then_inc(pool_step, 1)
            pool.memset(eps_t[:, :], EPS)
            pool.memset(bin_f[:, EC:(FULL + 1) * CH], 0.0)
            pool.memset(zeros[:, :], 0.0)
            pool.memset(cnt_x[:, :, 4:CX], 1.0)
            pool.wait_ge(pool_step, 3)
            pool.memset(empty_row[:, 2 * ED:2 * ED + 1], -1.0).then_inc(empty_made, 2)
            pool.affine_select(out=ident[:, :], in_=ident[:, :], compare_op=ALU.not_equal, fill=1.0, base=0,
                               pattern=[[-1, P]], channel_multiplier=1)
            pool.affine_select(out=below[:, :], in_=ones[:, :], compare_op=ALU.is_gt, fill=0.0, base=0,
                               pattern=[[1, P]], channel_multiplier=-1)
            pool.iota(iota_i[:, :], pattern=[[1, NT]], base=0, channel_multiplier=0).then_inc(consts_ready, 1)

            def scatter(r, n):
                for c in range(n):
                    pool.indirect_dma_start(
                        out=sorted_rows, out_offset=bass.IndirectOffsetOnAxis(ap=slot_i[:, r, c:c + 1], axis=0),
                        in_=rows[:, r, c, :], in_offset=None).then_inc(scattered[r], 16)

            pool.wait_ge(slots_cleared, 16 * NB)
            with pool.Fori(0, FULL // 2) as it:
                for r in range(2):
                    pool.wait_ge(rows_built, 2 * it + (r + 1))
                    pool.sem_inc(pool_waited, 1)
                    scatter(r, CH)
            pool.wait_ge(rows_built, FULL + 1)
            scatter(0, CH_LAST)

            pool.wait_ge(cb_moved, 16 * CX)
            pool.memset(m_t[:, :, H:SW], 1.0).then_inc(m_init, 1)
            pool.wait_ge(q_stored, 16 * NB)

            def gather(turn, j):
                t = turn * UN + j
                g = j // GRP
                if j % GRP == 0:
                    pool.wait_ge(srt_loaded[g], 16 * turn + 16)
                if j % GRP == 0:
                    if not is_int(turn, 1):
                        pool.wait_ge(pre_ready, t + (GRP - NG))
                        pool.sem_inc(pool_waited, 1)
                at = (j % GRP) * ROW + ROW - 1
                pool.indirect_dma_start(
                    out=gath[:, j % NG, :], out_offset=None, in_=q_table,
                    in_offset=bass.IndirectOffsetOnAxis(ap=srt[:, g, at:at + 1].bitcast(I32), axis=0),
                ).then_inc(gathered[j % NG], 16)

            for j in range(UN):
                gather(0, j)
            with pool.Fori(1, NT // UN) as turn:
                for j in range(UN):
                    gather(turn, j)

            pool.wait_ge(s_added, NT)
            pool.wait_ge(cnt_ready, 1)

            def copy_sums(b, j):
                if not is_int(b, 2):
                    pool.wait_ge(sT_psum, b - 1)
                pool.tensor_copy(s_in[:, j % 2, 0:H], xs[:, bass.ds(b * SW, H)])
                pool.tensor_copy(s_in[:, j % 2, H:H + CX],
                                 cnt_x[:, bass.ds(b, 1), :].rearrange("p b c -> p (b c)")).then_inc(s_copied, 1)

            def finish(b, j, stored):
                r = j % 3
                pool.wait_ge(zd_ready, b + 1)
                pool.tensor_tensor(upd[:, r, :], upd[:, r, :], nn[:, r, :], ALU.add).then_inc(nzd_ready, 1)
                if stored is not None:
                    pool.wait_ge(o_stored[r], stored)
                pool.wait_ge(nzd_ready, b + 1)
                pool.tensor_tensor(o_t[:, r, :], upd[:, r, :], x_in[:, r, :], ALU.add).then_inc(o_ready, 1)

            def update_step(turn, j):
                b = turn * UB + j
                if not (isinstance(b, int) and b + 4 >= NB):
                    copy_sums(b + 4, j + 4)
                stored = turn * (16 * UB // 3) + 16 * (j // 3)
                finish(b, j, None if isinstance(stored, int) and stored == 0 else stored)

            for b in range(4):
                copy_sums(b, b)
            for j in range(UB):
                update_step(0, j)
            with pool.Fori(1, NB // UB - 1) as turn:
                for j in range(UB):
                    update_step(turn, j)
            for j in range(UB + 1):
                update_step(NB // UB - 1, j)

        @block.vector
        def _(dve):
            n_step = [0]

            def link(ins):
                n_step[0] += 1
                ins.then_inc(dve_step, 1)
                dve.wait_ge(dve_step, n_step[0])

            V = nc.vector
            dve.wait_ge(src_in, 16)
            link(V.tensor_scalar(tmp_i[:, :], src_i[:, :], 7, None, ALU.arith_shift_right))
            link(V.tensor_copy(bin_f[:, 0:EC], tmp_i[:, :]))
            for b in range(BINS):
                if b >= 2:
                    dve.wait_ge(counted, b - 1)
                V.tensor_scalar(junk[:, b % 2, :], bin_f[:, 0:EC], float(b), None, ALU.is_equal, ALU.add,
                                accum_out=counts[:, b:b + 1]).then_inc(counted, 1)
            link(V.tensor_scalar(tmp_i[:, :], src_i[:, :], P - 1, None, ALU.bitwise_and))
            dve.wait_ge(consts_ready, 1)
            V.tensor_copy(iota_f[:, :], iota_i[:, :])
            link(V.tensor_copy(loc_f[:, :], tmp_i[:, :]))
            dve.wait_ge(summed, 1)
            link(V.tensor_scalar(tiles_i[:, :], bank[0][:, 0:BINS], float(P - 1), None, ALU.add))
            link(V.tensor_scalar(tiles_i[:, :], tiles_i[:, :], 7, None, ALU.arith_shift_right))
            link(V.tensor_copy(tiles_f[:, :], tiles_i[:, :]))
            link(V.tensor_tensor_scan(tiles_end[:, :], ones[:, 0:BINS], tiles_f[:, :], 0.0, ALU.mult, ALU.add))
            V.tensor_scalar(last_tile[:, :], tiles_end[0:1, 0:NB], -1.0, 0.0, ALU.add, ALU.max).then_inc(last_tiles, 1)
            link(V.tensor_tensor(tile_start[:, :], tiles_end[:, :], tiles_f[:, :], ALU.subtract))
            link(V.memset(tile_start[:, NB:BINS], float(NT)))
            link(V.tensor_scalar(base[:, :], tile_start[:, :], float(P), -1.0, ALU.mult, ALU.add))
            link(V.tensor_tensor(base[:, :], base[:, :], bank[0][:, 64:64 + BINS], ALU.add))
            dve.wait_ge(dst_in, 16)

            def place(k, r, n, place_no):
                step = place_no * 3
                col = k * CH
                V.tensor_tensor(in_bin[:, :, 0:n], bin_f[:, bass.ds(col, n)].unsqueeze(1).to_broadcast([P, BINS, n]),
                                iota_f[:, 0:BINS].unsqueeze(2).to_broadcast([P, BINS, n]), ALU.is_equal
                                ).then_inc(place_step, 1)
                dve.wait_ge(place_step, step + 1)
                for b in range(BINS):
                    start = base[:, b:b + 1] if is_int(k, 1) else ranked[:, 1 - r, b, CH - 1:CH]
                    last = V.tensor_tensor_scan(ranked[:, r, b, 0:n], ones[:, 0:n], in_bin[:, b, 0:n], start,
                                                ALU.mult, ALU.add)
                last.then_inc(place_step, 1)
                dve.wait_ge(place_step, step + 2)
                V.tensor_tensor(picked[:, :, 0:n], in_bin[:, :, 0:n], ranked[:, r, :, 0:n], ALU.mult
                                ).then_inc(place_step, 1)
                dve.wait_ge(place_step, step + 3)
                V.tensor_reduce(slot_f[:, r, 0:n], picked[:, :, 0:n].rearrange("p b c -> p c b"),
                                mybir.AxisListType.X, ALU.add).then_inc(slots_ready, 1)

            def build(k, r, n, turn):
                if turn is not None:
                    dve.wait_ge(scattered[r], SCAT * turn)
                col = k * CH
                V.tensor_copy(rows[:, r, 0:n, 2 * ED], loc_f[:, bass.ds(col, n)])
                V.tensor_copy(rows[:, r, 0:n, 2 * ED + 1].bitcast(I32), dst_i[:, bass.ds(col, n)])
                dve.wait_ge(slots_ready, k + 1)
                V.tensor_copy(slot_i[:, r, 0:n], slot_f[:, r, 0:n])
                dve.wait_ge(hi_built, k + 1)
                V.tensor_tensor(rows[:, r, 0:n, ED:2 * ED], ea_in[:, r, 0:n, :], rows[:, r, 0:n, 0:ED],
                                ALU.subtract).then_inc(rows_built, 1)

            def node_block(b, first):
                dve.wait_ge(pq_psum, b + 1)
                if not first:
                    dve.wait_ge(p_done, b)
                V.tensor_tensor(p_tmp[:, :], bank[1][:, 0:H], b1_s[:, :], ALU.add).then_inc(p_ready, 1)
                V.tensor_copy(xs[:, bass.ds(b * SW, SW)], zeros[:, :])
                dve.wait_ge(gh_psum, b + 1)
                V.tensor_tensor(g_tmp[:, 0:512], bank[2][:, :], bhh_s[:, 0:512], ALU.add)
                V.tensor_tensor(g_tmp[:, 512:G3], bank[3][:, 0:256], bhh_s[:, 512:G3], ALU.add).then_inc(gh_ready, 1)
                dve.wait_ge(p_hi, b + 1)
                hi = p_tab[:, bass.ds(b * (2 * H), H)]
                V.tensor_tensor(p_tab[:, bass.ds(b * (2 * H) + H, H)], p_tmp[:, :], hi.bitcast(F32),
                                ALU.subtract).then_inc(p_done, 1)

            place(0, 0, CH, 0)
            build(0, 0, CH, None)
            place(1, 1, CH, 1)
            build(1, 1, CH, None)
            place(2, 0, CH, 2)
            dve.wait_ge(x_loaded, 16)
            for b in range(NB):
                last = V.bn_stats(stats[:, b, :], xs_b[:, b, 0:H])
            link(last)
            for b in range(NB):
                last = V.bn_aggr(mv[:, b, :], stats[:, b:b + 1, :])
            last.then_inc(var_ready, 1)
            dve.wait_ge(w_loaded, 16 * N_W)
            link(V.tensor_copy(w1c_hi[:, :], w1c_s[:, :]))
            V.tensor_tensor(w1c_lo[:, :], w1c_s[:, :], w1c_hi[:, :].bitcast(F32), ALU.subtract).then_inc(w1c_ready, 1)
            dve.wait_ge(std_ready, 1)
            link(V.reciprocal(rstd[:, :], rstd[:, :]))
            V.scalar_tensor_tensor(out=nmr[:, :], in0=mv[:, :, 0], scalar=-1.0, in1=rstd[:, :],
                                   op0=ALU.mult, op1=ALU.mult).then_inc(norm_ready, 1)
            for c in range(2):
                dve.wait_ge(wc_psum, c + 1)
                V.tensor_copy(wc_s[:, c, 0:512], bank[1 + 2 * c][:, :])
                V.tensor_copy(wc_s[:, c, 512:G3], bank[2 + 2 * c][:, 0:256])
            dve.wait_ge(wc_psum, 3)
            V.tensor_copy(cw_s[:, 0:512], bank[5][0:1, :])
            V.tensor_copy(cw_s[:, 512:G3], bank[6][0:1, 0:256]).then_inc(wc_ready, 1)
            dve.wait_ge(wc_ready, 1)
            for n, whole in ((0, cw_s), (2, bih_s)):
                last = V.tensor_copy(cwb[0:1, n, :].bitcast(F32R), whole[:, :])
            link(last)
            for n, whole in ((0, cw_s), (2, bih_s)):
                last = V.tensor_tensor(cwb[0:1, n + 1, :], whole[:, :], cwb[0:1, n, :], ALU.subtract)
            last.then_inc(cb_cut, 1)

            for b in range(2):
                node_block(b, b == 0)
            link(V.tensor_scalar(blk_f[:, :], iota_f[0:1, :], tile_start[0:1, 1:2], None, ALU.is_ge))
            for b in range(2, NB):
                link(V.scalar_tensor_tensor(out=blk_f[:, :], in0=iota_f[0:1, :], scalar=tile_start[0:1, b:b + 1],
                                            in1=blk_f[:, :], op0=ALU.is_ge, op1=ALU.add))
            V.tensor_scalar(off_p[:, :], blk_f[:, :], float(2 * H), None, ALU.mult)
            V.tensor_scalar(off_s[:, :], blk_f[:, :], float(SW), None, ALU.mult).then_inc(tabs_ready, 1)
            with dve.Fori(1, FULL // 2) as it:
                for r in range(2):
                    k = 2 * it + r
                    build(k, r, CH, it)
                    if r == 0:
                        place(k + 1, 1, CH, k + 1)
                    else:
                        place(k + 1, 0, CH, k + 1)
                    node_block(k, False)
            build(FULL, 0, CH_LAST, FULL // 2)
            node_block(FULL, False)

            def one_hot(turn, j):
                g = j // GRP
                if j % GRP == 0:
                    dve.wait_ge(srt_loaded[g], 16 * turn + 16)
                at = (j % GRP) * ROW + ROW - 2
                V.tensor_scalar(oh[:, j % 8, :], iota_f[:, 0:P], srt[:, g, at:at + 1], None, ALU.is_equal
                                ).then_inc(oh_ready, 1)

            def terms(turn, j):
                t = turn * UN + j
                dve.wait_ge(pre_psum, t + 1)
                dve.wait_ge(gathered[j], 16 * turn + 16)
                if not (isinstance(t, int) and t < 4):
                    dve.wait_ge(m_ready, t - 3)
                V.tensor_tensor(pre[:, j % 4, :], ps_pre[j % 4][:, 0:H], gath[:, j % NG, :], ALU.add
                                ).then_inc(pre_ready, 1)

            def add_sums(turn, j, off):
                t = turn * UN + j
                dve.wait_ge(seg_psum, t + 1)
                if not (isinstance(t, int) and t < 1):
                    dve.wait_ge(s_added, t)
                s = xs[:, bass.ds(off, SW)]
                V.tensor_tensor(s, s, ps_seg[j % 2][:, 0:SW], ALU.add).then_inc(s_added, 1)

            def offsets(turn, eng_type, tab, top):
                _, vals = nc.values_load_multi_w_load_instructions(
                    tab[0:1, bass.ds(turn * UN, UN)], engines=[eng_type], min_val=0, max_val=top,
                    skip_runtime_bounds_check_because="a block number of 0..NB-1 by its own computation")
                return vals

            def turn_of(turn, first, last):
                if first:
                    for j in range(4):
                        one_hot(turn, j)
                    for j in range(2):
                        terms(turn, j)
                offs = offsets(turn, mybir.EngineType.DVE, off_s, (NB - 1) * SW)
                for j in range(UN):
                    if not last or j + 4 < UN:
                        one_hot(turn + (j + 4) // UN, (j + 4) % UN)
                    if not last or j + 2 < UN:
                        terms(turn + (j + 2) // UN, (j + 2) % UN)
                    add_sums(turn, j, offs[j])

            dve.wait_ge(tabs_ready, 1)
            dve.wait_ge(p_done, NB)
            turn_of(0, True, False)
            with dve.Fori(1, NT // UN - 1) as turn:
                turn_of(turn, False, False)
            turn_of(NT // UN - 1, False, True)

            dve.wait_ge(s_added, NT)
            cnt = xs_b[:, :, H]
            for n in range(2):
                last = V.tensor_copy(cnt_x[:, :, n].bitcast(F32R), cnt)
            link(last)
            for n in range(2):
                last = V.tensor_tensor(cnt_x[:, :, 2 + n], cnt, cnt_x[:, :, n], ALU.subtract)
            last.then_inc(cnt_ready, 1)

            def gate_sums(b, j, loads):
                r = j % 3
                dve.wait_ge(gx_psum, b + 1)
                dve.wait_ge(xg_loaded[r], loads)
                if not is_int(b, 3):
                    dve.wait_ge(zd_ready, b - 2)
                V.tensor_tensor(rz[:, r, :], ps_rz[r][:, :], g_in[:, r, 0:512], ALU.add).then_inc(rz_sum, 1)

            def update_step(turn, j):
                b = turn * UB + j
                if not (isinstance(b, int) and b + 1 >= NB):
                    gate_sums(b + 1, j + 1, turn * (32 * UB // 3) + 32 * ((j + 1) // 3 + 1))
                r, q = j % 3, (j - 1) % 3
                here = not (isinstance(b, int) and b >= NB)
                before = not (isinstance(b, int) and b < 1)
                if here:
                    dve.wait_ge(rz_ready, b + 1)
                    if not is_int(b, 3):
                        dve.wait_ge(o_ready, b - 2)
                    V.tensor_tensor(nn[:, r, :], rz[:, r, 0:H], g_in[:, r, 512:G3], ALU.mult).then_inc(rn_ready, 1)
                if before:
                    dve.wait_ge(n_ready, b)
                    V.tensor_tensor(upd[:, q, :], g_in[:, q, G3:GW], nn[:, q, :], ALU.subtract).then_inc(hn_ready, 1)
                if here:
                    dve.wait_ge(rn_ready, b + 1)
                    V.tensor_tensor(nn[:, r, :], nn[:, r, :], ps_n[r][:, 0:H], ALU.add).then_inc(n_sum, 1)
                if before:
                    dve.wait_ge(hn_ready, b)
                    V.tensor_tensor(upd[:, q, :], upd[:, q, :], rz[:, q, H:2 * H], ALU.mult).then_inc(zd_ready, 1)

            gate_sums(0, 0, 32)
            for j in range(UB):
                update_step(0, j)
            with dve.Fori(1, NB // UB - 1) as turn:
                for j in range(UB):
                    update_step(turn, j)
            for j in range(UB + 2):
                update_step(NB // UB - 1, j)

        @block.scalar
        def _(act):
            A = nc.scalar
            def build(r, n, loads, turn):
                act.wait_ge(ea_loaded[r], loads)
                if turn is not None:
                    act.wait_ge(scattered[r], SCAT * turn)
                A.activation(rows[:, r, 0:n, 0:ED].bitcast(F32R), ea_in[:, r, 0:n, :], ACT.Copy
                             ).then_inc(hi_built, 1)

            def node_block(b, b1_, first):
                if not first:
                    act.wait_ge(g_stored, 16 * (b1_ - 1))
                A.activation(g_tmp[:, G3:GW], xs[:, bass.ds(b * SW, H)], ACT.Relu, bias=nmr[:, bass.ds(b, 1)],
                             scale=rstd[:, bass.ds(b, 1)]).then_inc(h_ready, 1)
                act.wait_ge(hT_psum, b1_)
                A.activation(hT[:, :, :], bank[0][:, 0:2 * P].rearrange("p (a b) -> p a b", a=2), ACT.Copy
                             ).then_inc(hT_ready, 1)
                act.wait_ge(pq_psum, b1_)
                if not first:
                    act.wait_ge(q_stored, 16 * (b1_ - 1))
                A.activation(q_tmp[:, :], bank[4][:, 0:H], ACT.Copy).then_inc(q_ready, 1)
                act.wait_ge(p_ready, b1_)
                A.activation(p_tab[:, bass.ds(b * (2 * H), H)], p_tmp[:, :], ACT.Copy).then_inc(p_hi, 1)
                act.wait_ge(q_ready, b1_)
                act.dma_start(q_v[:, bass.ds(b, 1), :].rearrange("p b f -> p (b f)"), q_tmp[:, :]
                              ).then_inc(q_stored, 16)
                act.wait_ge(gh_ready, b1_)
                act.wait_ge(h_ready, b1_)
                act.dma_start(spill_v[:, bass.ds(b, 1), :].rearrange("p b f -> p (b f)"), g_tmp[:, :]
                              ).then_inc(g_stored, 16)

            build(0, CH, 16, None)
            build(1, CH, 16, None)
            act.wait_ge(consts_ready, 1)
            act.wait_ge(var_ready, 1)
            A.activation(rstd[:, :], mv[:, :, 1], ACT.Sqrt, bias=eps_t[:, :]).then_inc(std_ready, 1)
            act.wait_ge(norm_ready, 1)
            node_block(0, 1, True)
            node_block(1, 2, False)
            with act.Fori(1, FULL // 2) as it:
                for r in range(2):
                    build(r, CH, 16 * it + 16, it)
                    node_block(2 * it + r, 2 * it + (r + 1), False)
            build(0, CH_LAST, 16 * (FULL // 2 + 1), FULL // 2)
            node_block(FULL, FULL + 1, False)
            act.wait_ge(m_init, 1)

            def copy_transposed(turn, j):
                act.wait_ge(tr_psum, turn * UN + (j + 1))
                A.activation(tT[:, j % 4, :], ps_tr[j % 2][:, 0:2 * P], ACT.Copy).then_inc(tT_ready, 1)

            def relu(turn, j):
                t = turn * UN + j
                act.wait_ge(pre_ready, t + 1)
                if not (isinstance(t, int) and t < 4):
                    act.wait_ge(seg_psum, t - 3)
                A.activation(m_t[:, j % 4, 0:H], pre[:, j % 4, :], ACT.Relu).then_inc(m_ready, 1)

            def turn_of(turn, first, last):
                if first:
                    for j in range(3):
                        copy_transposed(turn, j)
                    for j in range(2):
                        relu(turn, j)
                for j in range(UN):
                    if not last or j + 3 < UN:
                        copy_transposed(turn + (j + 3) // UN, (j + 3) % UN)
                    if not last or j + 2 < UN:
                        relu(turn + (j + 2) // UN, (j + 2) % UN)

            turn_of(0, True, False)
            with act.Fori(1, NT // UN - 1) as turn:
                turn_of(turn, False, False)
            turn_of(NT // UN - 1, False, True)

            def sums_T(b, j):
                act.wait_ge(sT_psum, b + 1)
                if not is_int(b, 2):
                    act.wait_ge(gx_psum, b - 1)
                A.activation(sT[:, j % 2, :], bank[j % 2][:, 0:2 * P], ACT.Copy)
                A.activation(cT[:, j % 2, :], bank[j % 2][0:CX, 2 * P:3 * P], ACT.Copy).then_inc(sT_ready, 1)

            def sigmoid(b, j):
                act.wait_ge(rz_sum, b + 1)
                A.activation(rz[:, j % 3, :], rz[:, j % 3, :], ACT.Sigmoid).then_inc(rz_ready, 1)

            def tanh(b, j):
                act.wait_ge(n_sum, b + 1)
                A.activation(nn[:, j % 3, :], nn[:, j % 3, :], ACT.Tanh).then_inc(n_ready, 1)

            def update_step(turn, j):
                b = turn * UB + j
                if not (isinstance(b, int) and b + 2 >= NB):
                    sums_T(b + 2, j + 2)
                if not (isinstance(b, int) and b + 1 >= NB):
                    sigmoid(b + 1, j + 1)
                tanh(b, j)

            sums_T(0, 0)
            sums_T(1, 1)
            sigmoid(0, 0)
            for j in range(UB):
                update_step(0, j)
            with act.Fori(1, NB // UB - 1) as turn:
                for j in range(UB):
                    update_step(turn, j)
            for j in range(UB + 1):
                update_step(NB // UB - 1, j)

        @block.tensor
        def _(pe):
            T = nc.tensor
            pe.wait_ge(consts_ready, 1)
            pe.wait_ge(counted, BINS)
            T.matmul(bank[0][:, 0:BINS], ones[:, :], counts[:, :], start=True, stop=True)
            T.matmul(bank[0][:, 64:64 + BINS], below[:, :], counts[:, :], start=True, stop=True).then_inc(summed, 1)
            pe.wait_ge(w_loaded, 16 * N_W)
            for k in range(2):
                for lo, n, bk in ((0, 512, bank[1 + 2 * k]), (512, 256, bank[2 + 2 * k])):
                    for c in range(2):
                        last = T.matmul(bk[:, 0:n], w2_s[:, c, k * P:(k + 1) * P], wih_s[:, c, lo:lo + n],
                                        start=(c == 0), stop=(c == 1))
                last.then_inc(wc_psum, 1)
            for lo, n, bk in ((0, 512, bank[5]), (512, 256, bank[6])):
                for c in range(2):
                    last = T.matmul(bk[0:1, 0:n], b2_s[:, c:c + 1], wih_s[:, c, lo:lo + n],
                                    start=(c == 0), stop=(c == 1))
            last.then_inc(wc_psum, 1)
            pe.wait_ge(wc_ready, 1)

            def node_block(b1_, first):
                pe.wait_ge(h_ready, b1_)
                for c in range(2):
                    last = T.transpose(bank[0][:, c * P:(c + 1) * P], g_tmp[:, G3 + c * P:G3 + (c + 1) * P], ident[:, :])
                last.then_inc(hT_psum, 1)
                pe.wait_ge(hT_ready, b1_)
                if not first:
                    pe.wait_ge(q_ready, b1_ - 1)
                    pe.wait_ge(p_ready, b1_ - 1)
                for lo, bk in ((0, bank[1]), (H, bank[4])):
                    for c in range(2):
                        last = T.matmul(bk[:, 0:H], hT[:, c, :], w1pq_s[:, c, lo:lo + H],
                                        start=(c == 0), stop=(c == 1))
                last.then_inc(pq_psum, 1)
                if not first:
                    pe.wait_ge(gh_ready, b1_ - 1)
                for lo, n, bk in ((0, 512, bank[2]), (512, 256, bank[3])):
                    for c in range(2):
                        last = T.matmul(bk[:, 0:n], hT[:, c, :], whh_s[:, c, lo:lo + n],
                                        start=(c == 0), stop=(c == 1))
                last.then_inc(gh_psum, 1)

            node_block(1, True)
            with pe.Fori(2, NB + 1) as b1_:
                node_block(b1_, False)

            pe.wait_ge(tabs_ready, 1)
            pe.wait_ge(p_done, NB)
            pe.wait_ge(gh_ready, NB)
            pe.wait_ge(w1c_ready, 1)

            def transposes(turn, j):
                t = turn * UN + j
                pe.wait_ge(oh_ready, t + 1)
                if not (isinstance(t, int) and t < 2):
                    pe.wait_ge(tT_ready, t - 1)
                g, at = j // GRP, (j % GRP) * ROW
                T.transpose(ps_tr[j % 2][:, 0:P], srt[:, g, at:at + P], ident[:, :])
                T.transpose(ps_tr[j % 2][:, P:2 * P], oh[:, j % 8, :], ident[:, :]).then_inc(tr_psum, 1)

            def terms(turn, j, off):
                t = turn * UN + j
                pe.wait_ge(tT_ready, t + 1)
                if not (isinstance(t, int) and t < 4):
                    pe.wait_ge(pre_ready, t - 3)
                acc = ps_pre[j % 4][:, 0:H]
                T.matmul(acc, tT[:, j % 4, 0:P], w1c_hi[:, :], start=True, stop=False)
                T.matmul(acc, tT[:, j % 4, 0:P], w1c_lo[:, :], start=False, stop=False)
                T.matmul(acc, tT[:, j % 4, P:2 * P], p_tab[:, bass.ds(off, H)], start=False, stop=False)
                T.matmul(acc, tT[:, j % 4, P:2 * P], p_tab[:, bass.ds(off + H, H)], start=False, stop=True
                         ).then_inc(pre_psum, 1)

            def node_sums(turn, j):
                t = turn * UN + j
                pe.wait_ge(m_ready, t + 1)
                if not (isinstance(t, int) and t < 2):
                    pe.wait_ge(s_added, t - 1)
                T.matmul(ps_seg[j % 2][:, 0:SW], oh[:, j % 8, :], m_t[:, j % 4, :], start=True, stop=True
                         ).then_inc(seg_psum, 1)

            def offsets(turn):
                _, vals = nc.values_load_multi_w_load_instructions(
                    off_p[0:1, bass.ds(turn * UN + 2, UN) if not isinstance(turn, int) or turn * UN + 2 + UN <= NT
                          else slice(turn * UN + 2, NT)],
                    engines=[mybir.EngineType.PE], min_val=0, max_val=(NB - 1) * 2 * H,
                    skip_runtime_bounds_check_because="a block number of 0..NB-1 by its own computation")
                return vals

            def turn_of(turn, first, last):
                if first:
                    _, head = nc.values_load_multi_w_load_instructions(
                        off_p[0:1, 0:2], engines=[mybir.EngineType.PE], min_val=0, max_val=(NB - 1) * 2 * H,
                        skip_runtime_bounds_check_because="a block number of 0..NB-1 by its own computation")
                    for j in range(3):
                        transposes(turn, j)
                        if j < 2:
                            terms(turn, j, head[j])
                offs = offsets(turn)
                for j in range(UN):
                    if not last or j + 3 < UN:
                        transposes(turn + (j + 3) // UN, (j + 3) % UN)
                    if not last or j + 2 < UN:
                        terms(turn + (j + 2) // UN, (j + 2) % UN, offs[j])
                    node_sums(turn, j)

            turn_of(0, True, False)
            with pe.Fori(1, NT // UN - 1) as turn:
                turn_of(turn, False, False)
            turn_of(NT // UN - 1, False, True)

            pe.wait_ge(s_added, NT)
            pe.wait_ge(cb_moved, 16 * CX)

            def sums_T(b, j):
                pe.wait_ge(s_copied, b + 1)
                if not is_int(b, 2):
                    pe.wait_ge(sT_ready, b - 1)
                for c in range(2):
                    T.transpose(bank[j % 2][:, c * P:(c + 1) * P], s_in[:, j % 2, c * P:(c + 1) * P], ident[:, :])
                T.transpose(bank[j % 2][0:CX, 2 * P:3 * P], s_in[:, j % 2, H:H + CX], ident[:, :]).then_inc(sT_psum, 1)

            def products(b, j):
                pe.wait_ge(sT_ready, b + 1)
                if not is_int(b, 3):
                    pe.wait_ge(n_sum, b - 2)
                r = j % 3
                for lo, n, bk in ((0, 512, ps_rz[r]), (512, 256, ps_n[r])):
                    for c in range(2):
                        T.matmul(bk[:, 0:n], sT[:, j % 2, c * P:(c + 1) * P], wc_s[:, c, lo:lo + n],
                                 start=(c == 0), stop=False)
                    last = T.matmul(bk[:, 0:n], cT[:, j % 2, :], cb_s[:, lo:lo + n], start=False, stop=True)
                last.then_inc(gx_psum, 1)

            def update_step(turn, j):
                b = turn * UB + j
                if not (isinstance(b, int) and b + 3 >= NB):
                    sums_T(b + 3, j + 3)
                if not (isinstance(b, int) and b + 2 >= NB):
                    products(b + 2, j + 2)

            sums_T(0, 0)
            sums_T(1, 1)
            products(0, 0)
            sums_T(2, 2)
            products(1, 1)
            for j in range(UB):
                update_step(0, j)
            with pe.Fori(1, NB // UB - 1) as turn:
                for j in range(UB):
                    update_step(turn, j)
            for j in range(UB + 1):
                update_step(NB // UB - 1, j)


def kernel(x, src, dst, edge_attr_64, L0_gnn_W1, L0_gnn_b1, L0_gnn_W2, L0_gnn_b2, L0_gnn_W_ih, L0_gnn_b_ih,
           L0_gnn_W_hh, L0_gnn_b_hh):
    import numpy as np
    import concourse.bacc as bacc
    from concourse.bass_utils import run_bass_kernel_spmd

    w1 = np.asarray(L0_gnn_W1)
    pad_n, pad_e = NODES_PAD - NODES, EDGES_PAD - EDGES
    arrays = {
        "x": np.pad(np.asarray(x), ((0, pad_n), (0, 0))),
        "src": np.pad(np.asarray(src), (0, pad_e), constant_values=NODES_PAD),
        "dst": np.pad(np.asarray(dst), (0, pad_e)),
        "ea": np.pad(np.asarray(edge_attr_64), ((0, pad_e), (0, 0))),
        "w1pq": np.concatenate([w1[:, 0:H].T, w1[:, H:2 * H].T], axis=1),
        "w1c": w1[:, 2 * H:].T,
        "w2": np.asarray(L0_gnn_W2),
        "wih": np.asarray(L0_gnn_W_ih).T,
        "whh": np.asarray(L0_gnn_W_hh).T,
        "b1": np.asarray(L0_gnn_b1), "b2": np.asarray(L0_gnn_b2),
        "bih": np.asarray(L0_gnn_b_ih), "bhh": np.asarray(L0_gnn_b_hh),
    }
    arrays = {k: np.ascontiguousarray(v) for k, v in arrays.items()}
    nc = bacc.Bacc("TRN2", target_bir_lowering=False, num_devices=1)
    args = [nc.dram_tensor(f"in_{k}", v.shape, mybir.dt.from_np(v.dtype), kind="ExternalInput").ap()
            for k, v in arrays.items()]
    out = nc.dram_tensor("out", (NODES_PAD, H), F32, kind="ExternalOutput").ap()
    gnn_layer(nc, *args, out)
    r = run_bass_kernel_spmd(nc, [{f"in_{k}": v for k, v in arrays.items()}], core_ids=[0])
    return r.results[0]["out"][0:NODES]
```

```python
import concourse.bass as bass
from concourse import mybir
from contextlib import ExitStack

F32 = mybir.dt.float32
F32R = mybir.dt.float32r
BF16 = mybir.dt.bfloat16
I32 = mybir.dt.int32
ALU = mybir.AluOpType
ACT = mybir.ActivationFunctionType

P = 128
NODES, EDGES, H, ED = 3125, 50000, 256, 64
G3 = 3 * H
NB = -(-NODES // P)
NODES_PAD = NB * P
EC = -(-EDGES // P)
EDGES_PAD = EC * P
BINS = NB + 1
CH = 16
FULL = EC // CH
CH_LAST = EC - FULL * CH
UN = 32
NT = -(-((EDGES + NB * (P - 1)) // P) // UN) * UN
TA = 3
RA = 5
OA = 7
GRP = 4
NG = 16
NGRP = NG // GRP
ROW = 2 * ED + 2
SW = H + 1
GW = G3 + H
EPS = 1e-5
UB = 6
BY_SP, BY_ACT = 9, 9
assert FULL == NB - 1 and FULL % 2 == 0 and NB % UB == 1 and UN % NG == 0


def gnn_layer(nc, x, src, dst, ea, w1pq, w1c, w2, wih, whh, b1, b2, bih, bhh, out):
    ctx = ExitStack()
    with ctx:
        def sb(name, shape, dt=F32):
            return ctx.enter_context(nc.sbuf_tensor(name, shape, dt))

        def sem(name):
            return ctx.enter_context(nc.semaphore(name))

        sorted_rows = nc.dram_tensor("sorted_rows", [(NT + 1 + NB) * P, ROW], F32, kind="Internal").ap()
        q_table = nc.dram_tensor("q_table", [NODES_PAD, H], F32, kind="Internal").ap()
        spill = nc.dram_tensor("spill", [NODES_PAD, GW], F32, kind="Internal").ap()

        ident = sb("ident", [P, P])
        ones = sb("ones", [P, P])
        below = sb("below", [P, P])
        zeros = sb("zeros", [P, SW])
        empty_row = sb("empty_row", [P, ROW])
        iota_i = sb("iota_i", [P, NT], I32)
        iota_f = sb("iota_f", [P, NT])
        eps_t = sb("eps_t", [P, 1])
        w1c_s = sb("w1c_s", [P, H])
        w1c_hi = sb("w1c_hi", [P, H], F32R)
        w1c_lo = sb("w1c_lo", [P, H], F32R)
        wih_s = sb("wih_s", [P, 2, G3])
        wc_s = sb("wc_s", [P, 2, G3])
        cb_s = sb("cb_s", [P, G3])
        bn_s = sb("bn_s", [2, H], F32R)
        ones_r = sb("ones_r", [2, P], F32R)
        b1_s = sb("b1_s", [P, H])
        bhh_s = sb("bhh_s", [P, G3])
        b2_s = sb("b2_s", [P, 2])

        room = sb("room", [P, 4608])
        w1pq_s = room[:, 0:1024].rearrange("p (c n) -> p c n", c=2)
        whh_s = room[:, 1024:2560].rearrange("p (c n) -> p c n", c=2)
        w2_s = room[:, 3584:4096].rearrange("p (c n) -> p c n", c=2)
        g_tmp = room[:, 2560:2560 + 2 * GW].rearrange("p (r n) -> p r n", r=2)
        x_in = room[:, 3072:3072 + 3 * H].rearrange("p (r n) -> p r n", r=3)

        src_i = sb("src_i", [P, EC], I32)
        dst_i = sb("dst_i", [P, EC], I32)
        tmp_i = sb("tmp_i", [P, EC], I32)
        bin_f = sb("bin_f", [P, (FULL + 1) * CH])
        loc_f = sb("loc_f", [P, EC])
        bin_b = sb("bin_b", [P, EC], BF16)
        junk = sb("junk", [P, 2, EC], BF16)
        in_bin = sb("in_bin", [P, BINS, CH])
        ranked = sb("ranked", [P, 2, BINS, CH])
        slot_f = sb("slot_f", [P, 2, CH])
        counts = sb("counts", [P, BINS])
        tiles_i = sb("tiles_i", [P, BINS], I32)
        tiles_f = sb("tiles_f", [P, BINS])
        tiles_end = sb("tiles_end", [P, BINS])
        tile_start = sb("tile_start", [P, BINS])
        base = sb("base", [P, BINS])
        last_tile = sb("last_tile", [P, NB], I32)
        behind = sb("behind", [P, NB])
        own_tile = sb("own_tile", [P, NB])
        part_i = sb("part_i", [P, 1], I32)
        part_f = sb("part_f", [P, 1])
        clear_i = sb("clear_i", [P, NB], I32)
        start_col = sb("start_col", [NB, 1])
        started = sb("started", [NB, NT])
        off_p = sb("off_p", [1, NT], I32)
        off_s = sb("off_s", [1, NT], I32)

        xs = sb("xs", [P, NB * SW])
        xs_b = xs[:, :].rearrange("p (b w) -> p b w", w=SW)
        stats = sb("stats", [P, NB, 6])
        mv = sb("mv", [P, NB, 2])
        rstd = sb("rstd", [P, NB])
        nmr = sb("nmr", [P, NB])

        p_tab = sb("p_tab", [P, NB * 2 * H], F32R)
        hT = sb("hT", [P, 2, P])
        p_tmp = sb("p_tmp", [P, H])
        q_tmp = sb("q_tmp", [P, H])
        slot_i = sb("slot_i", [P, 2, CH], I32)

        oh = sb("oh", [P, 8, P], F32R)
        srt = sb("srt", [P, NGRP, GRP * ROW])
        ident_r = sb("ident_r", [P, P], F32R)
        tT = sb("tT", [P, 4, 2 * P], F32R)
        arena = sb("arena", [P, 9280])

        def cut(at, *dims):
            n = 1
            for d in dims:
                n *= d
            names = " ".join("abc"[:len(dims)])
            v = arena[:, at:at + n]
            return v if len(dims) == 1 else v.rearrange(
                f"p ({names}) -> p {names}", **{c: d for c, d in zip("abc", dims)})

        rows = cut(0, 2, CH, ROW)
        ea_in = cut(4160, 2, CH, ED)
        bn_cut = cut(6208, 2, H)
        b2_wide = cut(6720, 2, P)
        gath = cut(0, NG, H)
        m_t = cut(6208, 4, SW)
        pre = cut(7240, 4, H)
        s_in = cut(0, 3, H)
        sT = cut(768, 3, H)
        rz = cut(1536, 3, 2 * H)
        nn = cut(3072, 3, H)
        upd = cut(3840, 3, H)
        o_t = cut(4608, 3, H)
        g_in = [room[:, r * GW:(r + 1) * GW] for r in range(3)] + [cut(5376 + r * GW, GW) for r in range(3)]
        bih_s = sb("bih_s", [P, G3])

        bank = [ctx.enter_context(nc.psum_tensor(f"bank{i}", [P, 512], F32)) for i in range(8)]
        ps_tr, ps_pre, ps_seg = bank[0:2], bank[2:6], bank[6:8]
        ps_rz, ps_n = bank[2:5], bank[5:8]

        src_in, dst_in, x_loaded = sem("src_in"), sem("dst_in"), sem("x_loaded")
        w_loaded = sem("w_loaded")
        empty_made, last_tiles = sem("empty_made"), sem("last_tiles")
        spare_cleared, slots_cleared = sem("spare_cleared"), sem("slots_cleared")
        pool_step, dve_step = sem("pool_step"), sem("dve_step")
        clear_ready, pool_cleared = sem("clear_ready"), sem("pool_cleared")
        consts_ready, ident_ready = sem("consts_ready"), sem("ident_ready")
        pool_waited = sem("pool_waited")
        counted, summed = sem("counted"), sem("summed")
        place_step, slots_ready = sem("place_step"), sem("slots_ready")
        var_ready, std_ready, norm_ready = sem("var_ready"), sem("std_ready"), sem("norm_ready")
        wc_psum, wc_ready = sem("wc_psum"), sem("wc_ready")
        w1c_ready = sem("w1c_ready")
        b2_ready, bn_cut_ready, bn_moved = sem("b2_ready"), sem("bn_cut_ready"), sem("bn_moved")
        ea_loaded = [sem(f"ea_loaded{r}") for r in range(2)]
        hi_built, rows_built = sem("hi_built"), sem("rows_built")
        scattered = [sem(f"scattered{r}") for r in range(2)]
        h_ready, hT_psum, hT_ready = sem("h_ready"), sem("hT_psum"), sem("hT_ready")
        pq_psum, gh_psum = sem("pq_psum"), sem("gh_psum")
        p_ready, p_hi, p_done = sem("p_ready"), sem("p_hi"), sem("p_done")
        q_ready, gh_ready = sem("q_ready"), sem("gh_ready")
        q_stored = sem("q_stored")
        g_stored = [sem(f"g_stored{r}") for r in range(2)]
        start_ready = sem("start_ready")
        col_psum, started_ready, blk_psum, tabs_ready = (
            sem("col_psum"), sem("started_ready"), sem("blk_psum"), sem("tabs_ready"))
        m_init = sem("m_init")
        srt_loaded = [sem(f"srt_loaded{g}") for g in range(NGRP)]
        gathered = [sem(f"gathered{g}") for g in range(NG)]
        oh_ready, tr_psum, tT_ready = sem("oh_ready"), sem("tr_psum"), sem("tT_ready")
        pre_psum, pre_ready, m_ready = sem("pre_psum"), sem("pre_ready"), sem("m_ready")
        seg_psum, s_added = sem("seg_psum"), sem("s_added")
        xu_loaded = [sem(f"xu_loaded{r}") for r in range(3)]
        gu_loaded = [sem(f"gu_loaded{r}") for r in range(UB)]
        s_copied, sT_psum, sT_ready = sem("s_copied"), sem("sT_psum"), sem("sT_ready")
        gx_read, hidden_ready = sem("gx_read"), sem("hidden_ready")
        rz_psum, gx_psum, rz_sum, rz_ready = sem("rz_psum"), sem("gx_psum"), sem("rz_sum"), sem("rz_ready")
        rn_ready, n_sum, n_ready = sem("rn_ready"), sem("n_sum"), sem("n_ready")
        hn_ready, zd_ready, nx_ready = sem("hn_ready"), sem("zd_ready"), sem("nx_ready")
        o_ready = sem("o_ready")
        o_stored = [sem(f"o_stored{r}") for r in range(3)]

        block = ctx.enter_context(nc.Block())

        SCAT = 16 * CH
        ea_v = ea.rearrange("(p c) d -> p c d", p=P)
        sorted_v = sorted_rows.rearrange("(t p) c -> p t c", p=P)
        x_v = x.rearrange("(b p) f -> p b f", p=P)
        q_v = q_table.rearrange("(b p) f -> p b f", p=P)
        spill_v = spill.rearrange("(b p) f -> p b f", p=P)
        out_v = out.rearrange("(b p) f -> p b f", p=P)
        N_W = 11

        def loads_of(turn, j):
            return turn * (16 * UN // NG) + 16 * (j // NG + 1)

        def is_int(v, low):
            return isinstance(v, int) and v < low

        @block.sync
        def _(sp):
            sp.dma_start(src_i[:, :], src.rearrange("(p c) -> p c", p=P)).then_inc(src_in, 16)
            sp.dma_start(dst_i[:, :], dst.rearrange("(p c) -> p c", p=P)).then_inc(dst_in, 16)
            for r in range(2):
                sp.dma_start(ea_in[:, r, :, :], ea_v[:, r * CH:(r + 1) * CH, :]).then_inc(ea_loaded[r], 16)
            sp.wait_ge(empty_made, 2)
            spare = EDGES_PAD // P
            sp.dma_start(sorted_v[:, spare:NT, :], empty_row[:, :].unsqueeze(1).to_broadcast([P, NT - spare, ROW])
                         ).then_inc(spare_cleared, 16)
            sp.wait_ge(last_tiles, 1)
            sp.wait_ge(spare_cleared, 16)
            _, last = nc.values_load_multi_w_load_instructions(
                last_tile[0:1, 0:BY_SP], engines=[mybir.EngineType.SP], min_val=0, max_val=NT + NB,
                skip_runtime_bounds_check_because="a tile number of 0..NT+NB by its own computation")
            for v in last:
                sp.dma_start(sorted_v[:, bass.ds(v, 1), :].rearrange("p t c -> p (t c)"), empty_row[:, :]
                             ).then_inc(slots_cleared, 16)
            sp.wait_ge(pool_cleared, 16 * (NB - BY_SP - BY_ACT))
            sp.dma_start(xs_b[:, :, 0:H], x_v).then_inc(x_loaded, 16)
            for tile_, view in (
                (w1pq_s[:, :, :], w1pq.rearrange("(c p) n -> p c n", p=P)),
                (w1c_s[0:ED, :], w1c), (w1c_s[ED:2 * ED, :], w1c),
                (w2_s[:, :, :], w2.rearrange("(c p) n -> p c n", p=P)),
                (wih_s[:, :, :], wih.rearrange("(c p) n -> p c n", p=P)),
                (whh_s[:, :, :], whh.rearrange("(c p) n -> p c n", p=P)),
                (b1_s[:, :], b1.rearrange("(a n) -> a n", a=1).to_broadcast([P, H])),
                (bhh_s[:, :], bhh.rearrange("(a n) -> a n", a=1).to_broadcast([P, G3])),
                (b2_s[:, 0:1], b2[0:P].rearrange("(p a) -> p a", a=1)),
                (b2_s[:, 1:2], b2[P:2 * P].rearrange("(p a) -> p a", a=1)),
                (bih_s[:, :], bih.rearrange("(a n) -> a n", a=1).to_broadcast([P, G3])),
            ):
                sp.dma_start(tile_, view).then_inc(w_loaded, 16)

            def load_edges(k, r, loaded):
                sp.wait_ge(rows_built, loaded)
                sp.dma_start(ea_in[:, r, :, :], ea_v[:, bass.ds(k * CH, CH), :]).then_inc(ea_loaded[r], 16)

            for k in (2, 3):
                load_edges(k, k % 2, k - 1)
            sp.wait_ge(bn_cut_ready, 1)
            for part in range(2):
                sp.dma_start(bn_s[part:part + 1, :].bitcast(F32), bn_cut[0:1, part, :]).then_inc(bn_moved, 16)
            with sp.Fori(2, FULL // 2) as it:
                for r in range(2):
                    load_edges(2 * it + r, r, 2 * it + r - 1)
            sp.wait_ge(rows_built, FULL - 1)
            sp.dma_start(ea_in[:, 0, 0:CH_LAST, :], ea_v[:, FULL * CH:EC, :]).then_inc(ea_loaded[0], 16)

            sp.wait_ge(scattered[0], SCAT * (FULL // 2) + 16 * CH_LAST)
            sp.wait_ge(scattered[1], SCAT * (FULL // 2))

            def load_group(turn, g):
                sp.dma_start(srt[:, g, :].rearrange("p (t c) -> p t c", t=GRP),
                             sorted_v[:, bass.ds(turn * NG + g * GRP, GRP), :]).then_inc(srt_loaded[g], 16)

            def load_x(b, r):
                sp.dma_start(x_in[:, r, :], x_v[:, bass.ds(b, 1), :].rearrange("p b f -> p (b f)")
                             ).then_inc(xu_loaded[r], 16)

            def load_gates(b, r):
                sp.dma_start(g_in[r], spill_v[:, bass.ds(b, 1), :].rearrange("p b f -> p (b f)")
                             ).then_inc(gu_loaded[r], 16)

            for g in range(NGRP):
                load_group(0, g)
            sp.wait_ge(g_stored[0], 16 * (NB - NB // 2))
            sp.wait_ge(g_stored[1], 16 * (NB // 2))
            sp.wait_ge(gh_psum, NB)

            def next_group(turn, g):
                sp.wait_ge(pre_ready, turn * NG + (g + 1) * GRP - NG)
                load_group(turn, g)

            for g in range(NGRP):
                next_group(1, g)
                if g < 3:
                    load_gates(g, g)
                    load_x(g, g)
            with sp.Fori(2, NT // NG) as turn:
                for g in range(NGRP):
                    next_group(turn, g)

            def serve_block(b, j):
                if not (isinstance(b, int) and b + UB >= NB):
                    sp.wait_ge(hn_ready, b + 1)
                    load_gates(b + UB, j)
                if not (isinstance(b, int) and b < 1):
                    q = (j - 1) % 3
                    sp.wait_ge(o_ready, b)
                    sp.dma_start(out_v[:, bass.ds(b - 1, 1), :].rearrange("p b f -> p (b f)"), o_t[:, q, :]
                                 ).then_inc(o_stored[q], 16)
                    if not (isinstance(b, int) and b + 2 >= NB):
                        load_x(b + 2, q)

            sp.wait_ge(s_added, NT)
            for b in range(3, UB):
                load_gates(b, b)
            for j in range(UB):
                serve_block(j, j)
            with sp.Fori(1, NB // UB - 1) as turn:
                for j in range(UB):
                    serve_block(turn * UB + j, j)
            for j in range(UB + 2):
                serve_block((NB // UB - 1) * UB + j, j % UB)
            for r in range(3):
                sp.wait_ge(o_stored[r], 16 * len(range(r, NB, 3)))

        @block.gpsimd
        def _(pool):
            pool.memset(empty_row[:, :], 0.0).then_inc(pool_step, 1)
            pool.memset(ident[:, :], 0.0).then_inc(pool_step, 1)
            pool.memset(ones[:, :], 1.0).then_inc(pool_step, 1)
            pool.memset(eps_t[:, :], EPS)
            pool.memset(bin_f[:, EC:(FULL + 1) * CH], 0.0)
            pool.memset(zeros[:, :], 0.0)
            pool.wait_ge(pool_step, 3)
            pool.memset(empty_row[:, 2 * ED:2 * ED + 1], -1.0).then_inc(empty_made, 2)
            pool.affine_select(out=ident[:, :], in_=ident[:, :], compare_op=ALU.not_equal, fill=1.0, base=0,
                               pattern=[[-1, P]], channel_multiplier=1)
            pool.affine_select(out=below[:, :], in_=ones[:, :], compare_op=ALU.is_gt, fill=0.0, base=0,
                               pattern=[[1, P]], channel_multiplier=-1)
            pool.iota(part_i[:, :], pattern=[[1, 1]], base=0, channel_multiplier=1)
            pool.iota(iota_i[:, :], pattern=[[1, NT]], base=0, channel_multiplier=0).then_inc(consts_ready, 1)

            def scatter(r, n):
                for c in range(n):
                    pool.indirect_dma_start(
                        out=sorted_rows, out_offset=bass.IndirectOffsetOnAxis(ap=slot_i[:, r, c:c + 1], axis=0),
                        in_=rows[:, r, c, :], in_offset=None).then_inc(scattered[r], 16)

            pool.wait_ge(clear_ready, 1)
            pool.wait_ge(spare_cleared, 16)
            for b in range(BY_SP + BY_ACT, NB):
                pool.indirect_dma_start(
                    out=sorted_rows, out_offset=bass.IndirectOffsetOnAxis(ap=clear_i[:, b:b + 1], axis=0),
                    in_=empty_row[:, :], in_offset=None).then_inc(pool_cleared, 16)
            pool.wait_ge(slots_cleared, 16 * (BY_SP + BY_ACT))
            pool.wait_ge(pool_cleared, 16 * (NB - BY_SP - BY_ACT))
            with pool.Fori(0, FULL // 2) as it:
                for r in range(2):
                    pool.wait_ge(rows_built, 2 * it + (r + 1))
                    pool.sem_inc(pool_waited, 1)
                    scatter(r, CH)
            pool.wait_ge(rows_built, FULL + 1)
            scatter(0, CH_LAST)

            pool.wait_ge(bn_moved, 32)
            pool.memset(m_t[:, :, H:SW], 1.0).then_inc(m_init, 1)
            pool.wait_ge(q_stored, 16 * NB)

            def gather(turn, j):
                slot = j % NG
                g = slot // GRP
                if slot % GRP == 0:
                    pool.wait_ge(srt_loaded[g], loads_of(turn, j))
                    if not isinstance(turn, int):
                        pool.sem_inc(pool_waited, 1)
                at = (slot % GRP) * ROW + ROW - 1
                pool.indirect_dma_start(
                    out=gath[:, slot, :], out_offset=None, in_=q_table,
                    in_offset=bass.IndirectOffsetOnAxis(ap=srt[:, g, at:at + 1].bitcast(I32), axis=0),
                ).then_inc(gathered[slot], 16)

            for j in range(UN):
                gather(0, j)
            with pool.Fori(1, NT // UN) as turn:
                for j in range(UN):
                    gather(turn, j)

            def finish(b, j, stored, loads):
                r = j % 3
                pool.wait_ge(n_ready, b + 1)
                pool.tensor_tensor(upd[:, r, :], g_in[j % UB][:, G3:GW], nn[:, r, :], ALU.subtract
                                   ).then_inc(hn_ready, 1)
                pool.wait_ge(xu_loaded[r], loads)
                if stored is not None:
                    pool.wait_ge(o_stored[r], stored)
                pool.tensor_tensor(o_t[:, r, :], nn[:, r, :], x_in[:, r, :], ALU.add).then_inc(nx_ready, 1)
                pool.wait_ge(zd_ready, b + 1)
                pool.wait_ge(nx_ready, b + 1)
                pool.tensor_tensor(o_t[:, r, :], o_t[:, r, :], upd[:, r, :], ALU.add).then_inc(o_ready, 1)

            def update_step(turn, j):
                b = turn * UB + j
                stored = turn * (16 * UB // 3) + 16 * (j // 3)
                finish(b, j, None if isinstance(stored, int) and stored == 0 else stored, stored + 16)

            for j in range(UB):
                update_step(0, j)
            with pool.Fori(1, NB // UB - 1) as turn:
                for j in range(UB):
                    update_step(turn, j)
            for j in range(UB + 1):
                update_step(NB // UB - 1, j)

        @block.vector
        def _(dve):
            n_step = [0]

            def link(ins):
                n_step[0] += 1
                ins.then_inc(dve_step, 1)
                dve.wait_ge(dve_step, n_step[0])

            V = nc.vector
            dve.wait_ge(src_in, 16)
            link(V.tensor_scalar(tmp_i[:, :], src_i[:, :], 7, None, ALU.arith_shift_right))
            link(V.tensor_copy(bin_b[:, :], tmp_i[:, :]))
            for b in range(BINS):
                if b >= 2:
                    dve.wait_ge(counted, b - 1)
                V.tensor_scalar(junk[:, b % 2, :], bin_b[:, :], float(b), None, ALU.is_equal, ALU.add,
                                accum_out=counts[:, b:b + 1]).then_inc(counted, 1)
            V.tensor_copy(bin_f[:, 0:EC], tmp_i[:, :])
            dve.wait_ge(consts_ready, 1)
            V.tensor_copy(iota_f[:, :], iota_i[:, :])
            link(V.tensor_copy(part_f[:, :], part_i[:, :]))
            V.tensor_copy(ones_r[:, :], ones[0:2, :])
            V.tensor_scalar(behind[:, :], iota_f[:, 0:NB], float(NT + 1), None, ALU.add)
            dve.wait_ge(summed, 1)
            link(V.tensor_scalar(tiles_i[:, :], bank[0][:, 0:BINS], float(P - 1), None, ALU.add))
            link(V.tensor_scalar(tiles_i[:, :], tiles_i[:, :], 7, None, ALU.arith_shift_right))
            link(V.tensor_copy(tiles_f[:, :], tiles_i[:, :]))
            V.scalar_tensor_tensor(out=own_tile[:, :], in0=tiles_f[:, 0:NB], scalar=0.0, in1=behind[:, :],
                                   op0=ALU.is_equal, op1=ALU.mult)
            link(V.tensor_tensor_scan(tiles_end[:, :], ones[:, 0:BINS], tiles_f[:, :], 0.0, ALU.mult, ALU.add))
            V.scalar_tensor_tensor(out=last_tile[:, :], in0=tiles_end[:, 0:NB], scalar=-1.0, in1=own_tile[:, :],
                                   op0=ALU.add, op1=ALU.max).then_inc(last_tiles, 1)
            dve.wait_ge(last_tiles, 1)
            V.tensor_scalar(clear_i[:, :], last_tile[:, :], float(P), part_f[:, :], ALU.mult, ALU.add
                            ).then_inc(clear_ready, 1)
            link(V.tensor_tensor(tile_start[:, :], tiles_end[:, :], tiles_f[:, :], ALU.subtract))
            V.memset(tile_start[:, NB:BINS], float(NT)).then_inc(start_ready, 1)
            dve.wait_ge(start_ready, 1)
            link(V.tensor_scalar(base[:, :], tile_start[:, :], float(P), -1.0, ALU.mult, ALU.add))
            link(V.tensor_tensor(base[:, :], base[:, :], bank[0][:, 64:64 + BINS], ALU.add))
            dve.wait_ge(dst_in, 16)

            def place(k, r, n, place_no):
                step = place_no * 3
                col = k * CH
                V.tensor_tensor(in_bin[:, :, 0:n], bin_f[:, bass.ds(col, n)].unsqueeze(1).to_broadcast([P, BINS, n]),
                                iota_f[:, 0:BINS].unsqueeze(2).to_broadcast([P, BINS, n]), ALU.is_equal
                                ).then_inc(place_step, 1)
                dve.wait_ge(place_step, step + 1)
                for b in range(BINS):
                    start = base[:, b:b + 1] if is_int(k, 1) else ranked[:, 1 - r, b, CH - 1:CH]
                    last = V.tensor_tensor_scan(ranked[:, r, b, 0:n], ones[:, 0:n], in_bin[:, b, 0:n], start,
                                                ALU.mult, ALU.add)
                last.then_inc(place_step, 1)
                dve.wait_ge(place_step, step + 2)
                V.tensor_tensor(in_bin[:, :, 0:n], in_bin[:, :, 0:n], ranked[:, r, :, 0:n], ALU.mult
                                ).then_inc(place_step, 1)
                dve.wait_ge(place_step, step + 3)
                V.tensor_reduce(slot_f[:, r, 0:n], in_bin[:, :, 0:n].rearrange("p b c -> p c b"),
                                mybir.AxisListType.X, ALU.add).then_inc(slots_ready, 1)

            def build(k, r, n, turn):
                if turn is not None:
                    dve.wait_ge(scattered[r], SCAT * turn)
                col = k * CH
                V.tensor_copy(rows[:, r, 0:n, 2 * ED], loc_f[:, bass.ds(col, n)])
                V.tensor_copy(rows[:, r, 0:n, 2 * ED + 1].bitcast(I32), dst_i[:, bass.ds(col, n)])
                dve.wait_ge(slots_ready, k + 1)
                V.tensor_copy(slot_i[:, r, 0:n], slot_f[:, r, 0:n])
                dve.wait_ge(hi_built, k + 1)
                V.tensor_tensor(rows[:, r, 0:n, ED:2 * ED], ea_in[:, r, 0:n, :], rows[:, r, 0:n, 0:ED],
                                ALU.subtract).then_inc(rows_built, 1)

            def node_block(b, r, first):
                dve.wait_ge(pq_psum, b + 1)
                if not first:
                    dve.wait_ge(p_done, b)
                V.tensor_tensor(p_tmp[:, :], bank[1][:, 0:H], b1_s[:, :], ALU.add).then_inc(p_ready, 1)
                V.tensor_copy(xs[:, bass.ds(b * SW, SW)], zeros[:, :])
                dve.wait_ge(gh_psum, b + 1)
                V.tensor_tensor(g_tmp[:, r, 0:512], bank[2][:, :], bhh_s[:, 0:512], ALU.add)
                V.tensor_tensor(g_tmp[:, r, 512:G3], bank[3][:, 0:256], bhh_s[:, 512:G3], ALU.add).then_inc(gh_ready, 1)
                dve.wait_ge(p_hi, b + 1)
                hi = p_tab[:, bass.ds(b * (2 * H), H)]
                V.tensor_tensor(p_tab[:, bass.ds(b * (2 * H) + H, H)], p_tmp[:, :], hi.bitcast(F32),
                                ALU.subtract).then_inc(p_done, 1)

            place(0, 0, CH, 0)
            link(V.tensor_scalar(tmp_i[:, :], src_i[:, :], P - 1, None, ALU.bitwise_and))
            V.tensor_copy(ident_r[:, :], ident[:, :]).then_inc(ident_ready, 1)
            link(V.tensor_copy(loc_f[:, :], tmp_i[:, :]))
            build(0, 0, CH, None)
            place(1, 1, CH, 1)
            build(1, 1, CH, None)
            place(2, 0, CH, 2)
            dve.wait_ge(x_loaded, 16)
            for b in range(NB):
                last = V.bn_stats(stats[:, b, :], xs_b[:, b, 0:H])
            link(last)
            for b in range(NB):
                last = V.bn_aggr(mv[:, b, :], stats[:, b:b + 1, :])
            last.then_inc(var_ready, 1)
            dve.wait_ge(w_loaded, 16 * N_W)
            V.tensor_copy(b2_wide[:, :, :], b2_s[:, :].unsqueeze(2).to_broadcast([P, 2, P])).then_inc(b2_ready, 1)
            link(V.tensor_copy(w1c_hi[:, :], w1c_s[:, :]))
            V.tensor_tensor(w1c_lo[:, :], w1c_s[:, :], w1c_hi[:, :].bitcast(F32), ALU.subtract).then_inc(w1c_ready, 1)
            dve.wait_ge(std_ready, 1)
            link(V.reciprocal(rstd[:, :], rstd[:, :]))
            V.scalar_tensor_tensor(out=nmr[:, :], in0=mv[:, :, 0], scalar=-1.0, in1=rstd[:, :],
                                   op0=ALU.mult, op1=ALU.mult).then_inc(norm_ready, 1)
            build(2, 0, CH, 1)
            place(3, 1, CH, 3)
            for c in range(2):
                dve.wait_ge(wc_psum, c + 1)
                V.tensor_copy(wc_s[:, c, 0:512], bank[1 + 2 * c][:, :])
                V.tensor_copy(wc_s[:, c, 512:G3], bank[2 + 2 * c][:, 0:256])
            dve.wait_ge(wc_psum, 3)
            V.tensor_copy(cb_s[:, 0:512], bank[5][:, :])
            V.tensor_copy(cb_s[:, 512:G3], bank[6][:, 0:256]).then_inc(wc_ready, 1)
            V.tensor_copy(bn_cut[0:1, 0, :].bitcast(F32R), bih_s[0:1, 512:G3])
            link(V.tensor_tensor(bhh_s[:, 0:512], bhh_s[:, 0:512], bih_s[:, 0:512], ALU.add))
            V.tensor_tensor(bn_cut[0:1, 1, :], bih_s[0:1, 512:G3], bn_cut[0:1, 0, :], ALU.subtract
                            ).then_inc(bn_cut_ready, 1)

            dve.wait_ge(col_psum, 1)
            link(V.tensor_copy(start_col[:, :], bank[7][0:NB, 0:1]))
            V.tensor_scalar(started[:, :], iota_f[0:NB, :], start_col[:, :], None, ALU.is_ge).then_inc(started_ready, 1)
            build(3, 1, CH, 1)
            place(4, 0, CH, 4)
            node_block(0, 0, True)
            dve.wait_ge(blk_psum, 1)
            V.tensor_scalar(off_p[:, :], bank[7][0:1, 0:NT], -1.0, float(2 * H), ALU.add, ALU.mult)
            V.tensor_scalar(off_s[:, :], bank[7][0:1, 0:NT], -1.0, float(SW), ALU.add, ALU.mult).then_inc(tabs_ready, 1)
            for k in (4, 5):
                build(k, k % 2, CH, 2)
                place(k + 1, (k + 1) % 2, CH, k + 1)
                for b in (2 * k - 7, 2 * k - 6):
                    node_block(b, b % 2, False)
            with dve.Fori(3, FULL // 2) as it:
                for r in range(2):
                    k = 2 * it + r
                    build(k, r, CH, it)
                    place(k + 1, 1 - r, CH, k + 1)
                    node_block(k - 1, 1 - r, False)
            build(FULL, 0, CH_LAST, FULL // 2)
            for b in range(NB - 2, NB):
                node_block(b, b % 2, False)

            def one_hot(turn, j):
                g = j % NG // GRP
                if j % GRP == 0:
                    dve.wait_ge(srt_loaded[g], loads_of(turn, j))
                at = (j % GRP) * ROW + ROW - 2
                V.tensor_scalar(oh[:, j % 8, :], iota_f[:, 0:P], srt[:, g, at:at + 1], None, ALU.is_equal
                                ).then_inc(oh_ready, 1)

            def terms(turn, j):
                t = turn * UN + j
                dve.wait_ge(pre_psum, t + 1)
                dve.wait_ge(gathered[j % NG], loads_of(turn, j))
                V.tensor_tensor(pre[:, j % 4, :], ps_pre[j % 4][:, 0:H], gath[:, j % NG, :], ALU.add
                                ).then_inc(pre_ready, 1)

            def add_sums(turn, j, off):
                t = turn * UN + j
                dve.wait_ge(seg_psum, t + 1)
                if not (isinstance(t, int) and t < 1):
                    dve.wait_ge(s_added, t)
                s = xs[:, bass.ds(off, SW)]
                V.tensor_tensor(s, s, ps_seg[j % 2][:, 0:SW], ALU.add).then_inc(s_added, 1)

            def offsets(turn, eng_type, tab, top):
                _, vals = nc.values_load_multi_w_load_instructions(
                    tab[0:1, bass.ds(turn * UN, UN)], engines=[eng_type], min_val=0, max_val=top,
                    skip_runtime_bounds_check_because="a block number of 0..NB-1 by its own computation")
                return vals

            def turn_of(turn, first, last):
                if first:
                    for j in range(OA):
                        one_hot(turn, j)
                    for j in range(TA):
                        terms(turn, j)
                offs = offsets(turn, mybir.EngineType.DVE, off_s, (NB - 1) * SW)
                for j in range(UN):
                    if not last or j + OA < UN:
                        one_hot(turn + (j + OA) // UN, (j + OA) % UN)
                    if not last or j + TA < UN:
                        terms(turn + (j + TA) // UN, (j + TA) % UN)
                    add_sums(turn, j, offs[j])

            dve.wait_ge(tabs_ready, 1)
            dve.wait_ge(p_done, NB)
            turn_of(0, True, False)
            with dve.Fori(1, NT // UN - 1) as turn:
                turn_of(turn, False, False)
            turn_of(NT // UN - 1, False, True)

            dve.wait_ge(s_added, NT)

            def hidden_part(b, j, turn):
                dve.wait_ge(gu_loaded[j], 16 * turn + 16)
                g = g_in[j][:, 0:512]
                V.scalar_tensor_tensor(out=g, in0=cb_s[:, 0:512], scalar=xs[:, bass.ds(b * SW + H, 1)], in1=g,
                                       op0=ALU.mult, op1=ALU.add).then_inc(hidden_ready, 1)

            def update_step(turn, j):
                b = turn * UB + j
                r, q = j % 3, (j - 1) % 3
                known = isinstance(b, int)
                here = not (known and b >= NB)
                if here:
                    if not is_int(b, 3):
                        dve.wait_ge(o_ready, b - 2)
                    dve.wait_ge(rz_psum, b + 1)
                    dve.wait_ge(hidden_ready, b + 1)
                    V.tensor_tensor(rz[:, r, :], ps_rz[r][:, :], g_in[j % UB][:, 0:512], ALU.add).then_inc(rz_sum, 1)
                    dve.wait_ge(gx_psum, b + 1)
                    V.scalar_tensor_tensor(out=nn[:, r, :], in0=cb_s[:, 512:G3], scalar=xs[:, bass.ds(b * SW + H, 1)],
                                           in1=ps_n[r][:, 0:H], op0=ALU.mult, op1=ALU.add).then_inc(gx_read, 1)
                    if not (known and b + 1 >= NB):
                        hidden_part(b + 1, (j + 1) % UB, turn + (j + 1) // UB)
                    dve.wait_ge(rz_ready, b + 1)
                    V.tensor_tensor(upd[:, r, :], rz[:, r, 0:H], g_in[j % UB][:, 512:G3], ALU.mult
                                    ).then_inc(rn_ready, 1)
                if not (known and b < 1):
                    dve.wait_ge(hn_ready, b)
                    V.tensor_tensor(upd[:, q, :], upd[:, q, :], rz[:, q, H:2 * H], ALU.mult).then_inc(zd_ready, 1)
                if here:
                    dve.wait_ge(rn_ready, b + 1)
                    dve.wait_ge(gx_read, b + 1)
                    V.tensor_tensor(nn[:, r, :], nn[:, r, :], upd[:, r, :], ALU.add).then_inc(n_sum, 1)

            hidden_part(0, 0, 0)
            for j in range(UB):
                update_step(0, j)
            with dve.Fori(1, NB // UB - 1) as turn:
                for j in range(UB):
                    update_step(turn, j)
            for j in range(UB + 2):
                update_step(NB // UB - 1, j)

        @block.scalar
        def _(act):
            A = nc.scalar
            def build(r, n, loads, turn):
                act.wait_ge(ea_loaded[r], loads)
                if turn is not None:
                    act.wait_ge(scattered[r], SCAT * turn)
                A.activation(rows[:, r, 0:n, 0:ED].bitcast(F32R), ea_in[:, r, 0:n, :], ACT.Copy
                             ).then_inc(hi_built, 1)

            def normalize(b, r, stored):
                if stored is not None:
                    act.wait_ge(g_stored[r], stored)
                A.activation(g_tmp[:, r, G3:GW], xs[:, bass.ds(b * SW, H)], ACT.Relu, bias=nmr[:, bass.ds(b, 1)],
                             scale=rstd[:, bass.ds(b, 1)]).then_inc(h_ready, 1)

            def node_block(b, r, pair, first=False, last=False):
                act.wait_ge(hT_psum, b + 1)
                A.activation(hT[:, :, :], bank[0][:, 0:2 * P].rearrange("p (a b) -> p a b", a=2), ACT.Copy
                             ).then_inc(hT_ready, 1)
                if not last:
                    normalize(b + 1, 1 - r, None if first else 16 * (pair + r))
                act.wait_ge(pq_psum, b + 1)
                if not first:
                    act.wait_ge(q_stored, 16 * b)
                A.activation(q_tmp[:, :], bank[4][:, 0:H], ACT.Copy).then_inc(q_ready, 1)
                act.wait_ge(p_ready, b + 1)
                A.activation(p_tab[:, bass.ds(b * (2 * H), H)], p_tmp[:, :], ACT.Copy).then_inc(p_hi, 1)
                act.wait_ge(q_ready, b + 1)
                act.dma_start(q_v[:, bass.ds(b, 1), :].rearrange("p b f -> p (b f)"), q_tmp[:, :]
                              ).then_inc(q_stored, 16)
                act.wait_ge(gh_ready, b + 1)
                act.wait_ge(h_ready, b + 1)
                act.dma_start(spill_v[:, bass.ds(b, 1), :].rearrange("p b f -> p (b f)"), g_tmp[:, r, :]
                              ).then_inc(g_stored[r], 16)

            build(0, CH, 16, None)
            build(1, CH, 16, None)
            act.wait_ge(last_tiles, 1)
            act.wait_ge(spare_cleared, 16)
            _, last = nc.values_load_multi_w_load_instructions(
                last_tile[0:1, BY_SP:BY_SP + BY_ACT], engines=[mybir.EngineType.Activation], min_val=0,
                max_val=NT + NB, skip_runtime_bounds_check_because="a tile number of 0..NT+NB by its own computation")
            for v in last:
                act.dma_start(sorted_v[:, bass.ds(v, 1), :].rearrange("p t c -> p (t c)"), empty_row[:, :]
                              ).then_inc(slots_cleared, 16)
            act.wait_ge(consts_ready, 1)
            act.wait_ge(var_ready, 1)
            A.activation(rstd[:, :], mv[:, :, 1], ACT.Sqrt, bias=eps_t[:, :]).then_inc(std_ready, 1)
            act.wait_ge(norm_ready, 1)
            build(0, CH, 32, 1)
            normalize(0, 0, None)
            build(1, CH, 32, 1)
            node_block(0, 0, 0, first=True)
            for k in (4, 5):
                build(k % 2, CH, 48, 2)
                for b in (2 * k - 7, 2 * k - 6):
                    node_block(b, b % 2, b // 2)
            with act.Fori(3, FULL // 2) as it:
                for r in range(2):
                    build(r, CH, 16 * it + 16, it)
                    node_block(2 * it + (r - 1), 1 - r, it + (r - 1))
            build(0, CH_LAST, 16 * (FULL // 2 + 1), FULL // 2)
            for b in range(NB - 2, NB):
                node_block(b, b % 2, b // 2, last=b == NB - 1)
            A.activation(nmr[:, 0:1], nmr[:, 0:1], ACT.Sigmoid)
            act.wait_ge(m_init, 1)

            def copy_transposed(turn, j):
                act.wait_ge(tr_psum, turn * UN + (j + 1))
                A.activation(tT[:, j % 4, :], ps_tr[j % 2][:, 0:2 * P], ACT.Copy).then_inc(tT_ready, 1)

            def relu(turn, j):
                t = turn * UN + j
                act.wait_ge(pre_ready, t + 1)
                A.activation(m_t[:, j % 4, 0:H], pre[:, j % 4, :], ACT.Relu).then_inc(m_ready, 1)

            def turn_of(turn, first, last):
                if first:
                    for j in range(RA):
                        copy_transposed(turn, j)
                    for j in range(TA):
                        relu(turn, j)
                for j in range(UN):
                    if not last or j + RA < UN:
                        copy_transposed(turn + (j + RA) // UN, (j + RA) % UN)
                    if not last or j + TA < UN:
                        relu(turn + (j + TA) // UN, (j + TA) % UN)

            turn_of(0, True, False)
            with act.Fori(1, NT // UN - 1) as turn:
                turn_of(turn, False, False)
            turn_of(NT // UN - 1, False, True)

            act.wait_ge(s_added, NT)

            def copy_sums(b, j):
                if not is_int(b, 3):
                    act.wait_ge(sT_psum, b - 2)
                A.activation(s_in[:, j % 3, :], xs[:, bass.ds(b * SW, H)], ACT.Copy).then_inc(s_copied, 1)

            def sums_T(b, j):
                act.wait_ge(sT_psum, b + 1)
                if not is_int(b, 3):
                    act.wait_ge(gx_psum, b - 2)
                A.activation(sT[:, j % 3, :], bank[j % 2][:, 0:2 * P], ACT.Copy).then_inc(sT_ready, 1)

            def sigmoid(b, j):
                act.wait_ge(rz_sum, b + 1)
                A.activation(rz[:, j % 3, :], rz[:, j % 3, :], ACT.Sigmoid).then_inc(rz_ready, 1)

            def tanh(b, j):
                act.wait_ge(n_sum, b + 1)
                A.activation(nn[:, j % 3, :], nn[:, j % 3, :], ACT.Tanh).then_inc(n_ready, 1)

            def update_step(turn, j):
                b = turn * UB + j
                sigmoid(b, j)
                if not (isinstance(b, int) and b + 3 >= NB):
                    sums_T(b + 3, j + 3)
                if not (isinstance(b, int) and b + 5 >= NB):
                    copy_sums(b + 5, j + 5)
                tanh(b, j)

            for b in range(2):
                copy_sums(b, b)
            for b in range(3):
                sums_T(b, b)
                copy_sums(b + 2, b + 2)
            for j in range(UB):
                update_step(0, j)
            with act.Fori(1, NB // UB - 1) as turn:
                for j in range(UB):
                    update_step(turn, j)
            for j in range(UB + 1):
                update_step(NB // UB - 1, j)

        @block.tensor
        def _(pe):
            T = nc.tensor
            pe.wait_ge(consts_ready, 1)
            pe.wait_ge(counted, BINS)
            T.matmul(bank[0][:, 0:BINS], ones[:, :], counts[:, :], start=True, stop=True)
            T.matmul(bank[0][:, 64:64 + BINS], below[:, :], counts[:, :], start=True, stop=True).then_inc(summed, 1)
            pe.wait_ge(start_ready, 1)
            T.matmul(bank[7][0:NB, 0:1], tile_start[0:1, 0:NB], ones[0:1, 0:1], start=True, stop=True
                     ).then_inc(col_psum, 1)
            pe.wait_ge(w_loaded, 16 * N_W)
            for k in range(2):
                for lo, n, bk in ((0, 512, bank[1 + 2 * k]), (512, 256, bank[2 + 2 * k])):
                    for c in range(2):
                        last = T.matmul(bk[:, 0:n], w2_s[:, c, k * P:(k + 1) * P], wih_s[:, c, lo:lo + n],
                                        start=(c == 0), stop=(c == 1))
                last.then_inc(wc_psum, 1)
            pe.wait_ge(b2_ready, 1)
            for lo, n, bk in ((0, 512, bank[5]), (512, 256, bank[6])):
                for c in range(2):
                    last = T.matmul(bk[:, 0:n], b2_wide[:, c, :], wih_s[:, c, lo:lo + n],
                                    start=(c == 0), stop=(c == 1))
            last.then_inc(wc_psum, 1)
            pe.wait_ge(wc_ready, 1)

            pe.wait_ge(started_ready, 1)
            T.matmul(bank[7][0:1, 0:NT], ones[0:NB, 0:1], started[:, :], start=True, stop=True).then_inc(blk_psum, 1)

            def node_block(b1_, r, first):
                pe.wait_ge(h_ready, b1_)
                for c in range(2):
                    last = T.transpose(bank[0][:, c * P:(c + 1) * P], g_tmp[:, r, G3 + c * P:G3 + (c + 1) * P],
                                       ident[:, :])
                last.then_inc(hT_psum, 1)
                pe.wait_ge(hT_ready, b1_)
                if not first:
                    pe.wait_ge(q_ready, b1_ - 1)
                    pe.wait_ge(p_ready, b1_ - 1)
                for lo, bk in ((0, bank[1]), (H, bank[4])):
                    for c in range(2):
                        last = T.matmul(bk[:, 0:H], hT[:, c, :], w1pq_s[:, c, lo:lo + H],
                                        start=(c == 0), stop=(c == 1))
                last.then_inc(pq_psum, 1)
                if not first:
                    pe.wait_ge(gh_ready, b1_ - 1)
                for lo, n, bk in ((0, 512, bank[2]), (512, 256, bank[3])):
                    for c in range(2):
                        last = T.matmul(bk[:, 0:n], hT[:, c, :], whh_s[:, c, lo:lo + n],
                                        start=(c == 0), stop=(c == 1))
                last.then_inc(gh_psum, 1)

            node_block(1, 0, True)
            with pe.Fori(1, NB // 2 + 1) as pair:
                for r in range(2):
                    node_block(2 * pair + r, 1 - r, False)

            pe.wait_ge(tabs_ready, 1)
            pe.wait_ge(ident_ready, 1)
            pe.wait_ge(p_done, NB)
            pe.wait_ge(gh_ready, NB)
            pe.wait_ge(w1c_ready, 1)

            def transposes(turn, j):
                t = turn * UN + j
                pe.wait_ge(oh_ready, t + 1)
                if not (isinstance(t, int) and t < 2):
                    pe.wait_ge(tT_ready, t - 1)
                g, at = j % NG // GRP, (j % GRP) * ROW
                bk = ps_tr[j % 2]
                T.transpose(bk[:, 0:P].bitcast(F32R), srt[:, g, at:at + P].bitcast(F32R), ident_r[:, :])
                T.transpose(bk[:, P:2 * P].bitcast(F32R), oh[:, j % 8, :], ident_r[:, :]).then_inc(tr_psum, 1)

            def terms(turn, j, off):
                t = turn * UN + j
                pe.wait_ge(tT_ready, t + 1)
                acc = ps_pre[j % 4][:, 0:H]
                T.matmul(acc, tT[:, j % 4, 0:P], w1c_hi[:, :], start=True, stop=False)
                T.matmul(acc, tT[:, j % 4, 0:P], w1c_lo[:, :], start=False, stop=False)
                T.matmul(acc, tT[:, j % 4, P:2 * P], p_tab[:, bass.ds(off, H)], start=False, stop=False)
                T.matmul(acc, tT[:, j % 4, P:2 * P], p_tab[:, bass.ds(off + H, H)], start=False, stop=True
                         ).then_inc(pre_psum, 1)

            def node_sums(turn, j):
                t = turn * UN + j
                pe.wait_ge(m_ready, t + 1)
                if not (isinstance(t, int) and t < 2):
                    pe.wait_ge(s_added, t - 1)
                T.matmul(ps_seg[j % 2][:, 0:SW], oh[:, j % 8, :].bitcast(F32), m_t[:, j % 4, :], start=True, stop=True
                         ).then_inc(seg_psum, 1)

            def offsets(turn):
                _, vals = nc.values_load_multi_w_load_instructions(
                    off_p[0:1, bass.ds(turn * UN + TA, UN) if not isinstance(turn, int) or turn * UN + TA + UN <= NT
                          else slice(turn * UN + TA, NT)],
                    engines=[mybir.EngineType.PE], min_val=0, max_val=(NB - 1) * 2 * H,
                    skip_runtime_bounds_check_because="a block number of 0..NB-1 by its own computation")
                return vals

            def turn_of(turn, first, last):
                if first:
                    _, head = nc.values_load_multi_w_load_instructions(
                        off_p[0:1, 0:TA], engines=[mybir.EngineType.PE], min_val=0, max_val=(NB - 1) * 2 * H,
                        skip_runtime_bounds_check_because="a block number of 0..NB-1 by its own computation")
                    for j in range(RA):
                        transposes(turn, j)
                        if j >= RA - TA:
                            terms(turn, j + TA - RA, head[j + TA - RA])
                offs = offsets(turn)
                for j in range(UN):
                    if not last or j + RA < UN:
                        transposes(turn + (j + RA) // UN, (j + RA) % UN)
                    if not last or j + TA < UN:
                        terms(turn + (j + TA) // UN, (j + TA) % UN, offs[j])
                    node_sums(turn, j)

            turn_of(0, True, False)
            with pe.Fori(1, NT // UN - 1) as turn:
                turn_of(turn, False, False)
            turn_of(NT // UN - 1, False, True)

            pe.wait_ge(s_added, NT)
            pe.wait_ge(bn_moved, 32)

            def sums_T(b, j):
                pe.wait_ge(s_copied, b + 1)
                if not is_int(b, 2):
                    pe.wait_ge(sT_ready, b - 1)
                for c in range(2):
                    last = T.transpose(bank[j % 2][:, c * P:(c + 1) * P], s_in[:, j % 3, c * P:(c + 1) * P],
                                       ident[:, :])
                last.then_inc(sT_psum, 1)

            def products(b, j):
                pe.wait_ge(sT_ready, b + 1)
                if not is_int(b, 3):
                    pe.wait_ge(gx_read, b - 2)
                r = j % 3
                for c in range(2):
                    last = T.matmul(ps_rz[r][:, :], sT[:, r, c * P:(c + 1) * P], wc_s[:, c, 0:512],
                                    start=(c == 0), stop=(c == 1))
                last.then_inc(rz_psum, 1)
                for c in range(2):
                    T.matmul(ps_n[r][:, 0:H], sT[:, r, c * P:(c + 1) * P], wc_s[:, c, 512:G3],
                             start=(c == 0), stop=False)
                T.matmul(ps_n[r][:, 0:H], ones_r[:, :], bn_s[:, :], start=False, stop=True).then_inc(gx_psum, 1)

            def update_step(turn, j):
                b = turn * UB + j
                if not (isinstance(b, int) and b + 3 >= NB):
                    sums_T(b + 3, j + 3)
                if not (isinstance(b, int) and b + 1 >= NB):
                    products(b + 1, j + 1)

            for b in range(2):
                sums_T(b, b)
            products(0, 0)
            sums_T(2, 2)
            for j in range(UB):
                update_step(0, j)
            with pe.Fori(1, NB // UB - 1) as turn:
                for j in range(UB):
                    update_step(turn, j)
            for j in range(UB + 1):
                update_step(NB // UB - 1, j)


def kernel(x, src, dst, edge_attr_64, L0_gnn_W1, L0_gnn_b1, L0_gnn_W2, L0_gnn_b2, L0_gnn_W_ih, L0_gnn_b_ih,
           L0_gnn_W_hh, L0_gnn_b_hh):
    import numpy as np
    import concourse.bacc as bacc
    from concourse.bass_utils import run_bass_kernel_spmd

    w1 = np.asarray(L0_gnn_W1)
    pad_n, pad_e = NODES_PAD - NODES, EDGES_PAD - EDGES
    arrays = {
        "x": np.pad(np.asarray(x), ((0, pad_n), (0, 0))),
        "src": np.pad(np.asarray(src), (0, pad_e), constant_values=NODES_PAD),
        "dst": np.pad(np.asarray(dst), (0, pad_e)),
        "ea": np.pad(np.asarray(edge_attr_64), ((0, pad_e), (0, 0))),
        "w1pq": np.concatenate([w1[:, 0:H].T, w1[:, H:2 * H].T], axis=1),
        "w1c": w1[:, 2 * H:].T,
        "w2": np.asarray(L0_gnn_W2),
        "wih": np.asarray(L0_gnn_W_ih).T,
        "whh": np.asarray(L0_gnn_W_hh).T,
        "b1": np.asarray(L0_gnn_b1), "b2": np.asarray(L0_gnn_b2),
        "bih": np.asarray(L0_gnn_b_ih), "bhh": np.asarray(L0_gnn_b_hh),
    }
    arrays = {k: np.ascontiguousarray(v) for k, v in arrays.items()}
    nc = bacc.Bacc("TRN2", target_bir_lowering=False, num_devices=1)
    args = [nc.dram_tensor(f"in_{k}", v.shape, mybir.dt.from_np(v.dtype), kind="ExternalInput").ap()
            for k, v in arrays.items()]
    out = nc.dram_tensor("out", (NODES_PAD, H), F32, kind="ExternalOutput").ap()
    gnn_layer(nc, *args, out)
    r = run_bass_kernel_spmd(nc, [{f"in_{k}": v for k, v in arrays.items()}], core_ids=[0])
    return r.results[0]["out"][0:NODES]
```
